# Optimizing a Trainium2 kernel written in Bass

```python
import numpy as np
import jax
import jax.numpy as jnp

def _softmax(x, axis=-1):
    return jax.nn.softmax(x, axis=axis)

def _gelu(x):
    return jax.nn.gelu(x, approximate=True)

def _silu(x):
    return jax.nn.silu(x)

def _sigmoid(x):
    return jax.nn.sigmoid(x)

def _layernorm(x, axis=-1, eps=1e-05):
    m = jnp.mean(x, axis=axis, keepdims=True)
    v = jnp.var(x, axis=axis, keepdims=True)
    return (x - m) / jnp.sqrt(v + eps)

def _scatter_add(tgt, idx, src, axis=0):
    return tgt.at[idx].add(src)

def _segment_sum(src, seg, n):
    return jax.ops.segment_sum(src, seg, n)
kernel_name = 'mk_pixart_seq_d4_seqx_r8_d9be32'

def setup_inputs(seed: int=0):
    np.random.seed(seed)
    _w = jnp.asarray

    def _rec_inputs():
        import jax
        import jax.numpy as jnp
        _rk = jax.random.key(seed)
        x = -0.0002928 + 1 * jax.random.normal(jax.random.fold_in(_rk, 1), (8, 128, 128), jnp.float32)
        _lenS = 128 - jax.random.randint(jax.random.fold_in(_rk, 7), (8,), 0, max(1, 128 // 4) + 1, jnp.int32)
        _lenS2 = 128 - jax.random.randint(jax.random.fold_in(_rk, 8), (8,), 0, max(1, 128 // 4) + 1, jnp.int32)
        _ctx_768P = jax.random.normal(jax.random.fold_in(_rk, 11), (8, 16, 96), jnp.float32)
        _ctx_768c = jax.random.dirichlet(jax.random.fold_in(_rk, 511), 0.3 * jnp.ones((16,), jnp.float32), (8, 128))
        _ctx_768t = jnp.einsum('bsk,bkd->bsd', _ctx_768c, _ctx_768P)
        _ctx_768t = _ctx_768t * jax.lax.rsqrt(jnp.mean(jnp.square(_ctx_768t)) + 1e-12) * 0.953939
        ctx_768 = 0.00095986 + 0.999812 * (_ctx_768t + 0.3 * jax.random.normal(jax.random.fold_in(_rk, 611), (8, 128, 96), jnp.float32))
        cond_1024 = 0.0132156 + 1.00766 * jax.random.normal(jax.random.fold_in(_rk, 12), (8, 128), jnp.float32)
        return (x, ctx_768, cond_1024)
    x, ctx_768, cond_1024 = _rec_inputs()

    def _L0_xcond_setup():
        import jax, jax.numpy as jnp
        import numpy as np
        D = 128
        CD = 96
        H = 16
        HD = D // H
        EPS = 1e-05

        def _ln(x, w, b):
            m = jnp.mean(x, axis=-1, keepdims=True)
            v = jnp.var(x, axis=-1, keepdims=True)
            return (x - m) * jax.lax.rsqrt(v + EPS) * w + b

        def _attn(q, k, v):
            q = q.reshape(q.shape[0], q.shape[1], H, HD).transpose(0, 2, 1, 3)
            k = k.reshape(k.shape[0], k.shape[1], H, HD).transpose(0, 2, 1, 3)
            v = v.reshape(v.shape[0], v.shape[1], H, HD).transpose(0, 2, 1, 3)
            scores = jnp.einsum('bhnd,bhmd->bhnm', q, k) * HD ** (-0.5)
            p = jax.nn.softmax(scores, axis=-1)
            o = jnp.einsum('bhnm,bhmd->bhnd', p, v)
            return o.transpose(0, 2, 1, 3).reshape(o.shape[0], o.shape[2], D)
        key = jax.random.key(seed)
        ks = iter(jax.random.split(key, 32))
        s = 0.02
        inp = {'x': jax.random.normal(next(ks), (4, 128, D), jnp.float32), 'context': jax.random.normal(next(ks), (4, 32, CD), jnp.float32), 'time_emb': jax.random.normal(next(ks), (4, D), jnp.float32), 'ln1_w': jnp.ones((D,)), 'ln1_b': jnp.zeros((D,)), 'ln2_w': jnp.ones((D,)), 'ln2_b': jnp.zeros((D,)), 'ln3_w': jnp.ones((D,)), 'ln3_b': jnp.zeros((D,)), 'Wqkv': jax.random.normal(next(ks), (D, 3 * D)) * s, 'bqkv': jnp.zeros((3 * D,)), 'Wos': jax.random.normal(next(ks), (D, D)) * s, 'bos': jnp.zeros((D,)), 'Wq': jax.random.normal(next(ks), (D, D)) * s, 'bq': jnp.zeros((D,)), 'Wk': jax.random.normal(next(ks), (CD, D)) * s, 'bk': jnp.zeros((D,)), 'Wv': jax.random.normal(next(ks), (CD, D)) * s, 'bv': jnp.zeros((D,)), 'Woc': jax.random.normal(next(ks), (D, D)) * s, 'boc': jnp.zeros((D,)), 'W1': jax.random.normal(next(ks), (D, 4 * D)) * s, 'b1': jnp.zeros((4 * D,)), 'W2': jax.random.normal(next(ks), (4 * D, D)) * s, 'b2': jnp.zeros((D,)), 'Wmod': jax.random.normal(next(ks), (D, 6 * D)) * s, 'bmod': jnp.zeros((6 * D,))}
        return inp
    _L0_xcond_all = _L0_xcond_setup()
    _L0_xcond_in = {k: v for k, v in _L0_xcond_all.items() if k in ('ln1_w', 'ln1_b', 'ln2_w', 'ln2_b', 'ln3_w', 'ln3_b', 'Wqkv', 'bqkv', 'Wos', 'bos', 'Wq', 'bq', 'Wk', 'bk', 'Wv', 'bv', 'Woc', 'boc', 'W1', 'b1', 'W2', 'b2', 'Wmod', 'bmod')}
    del _L0_xcond_all

    def _L1_xcond_setup():
        import jax, jax.numpy as jnp
        import numpy as np
        B, N, M = (2, 128, 64)
        D, H, DH = (128, 16, 64)
        MID = H * DH
        DC = 96
        MULT = 4
        EPS = 1e-05

        def _ln(x, w, b):
            mu = jnp.mean(x, -1, keepdims=True)
            var = jnp.mean((x - mu) ** 2, -1, keepdims=True)
            return (x - mu) * jax.lax.rsqrt(var + EPS) * w + b

        def _sincos(n, d):
            inv = 1.0 / 10000.0 ** (jnp.arange(0, d, 2, dtype=jnp.float32) / d)
            ang = jnp.arange(n, dtype=jnp.float32)[:, None] * inv[None, :]
            return (jnp.sin(ang), jnp.cos(ang))

        def _rope(x, sin, cos):
            s = sin[None, None]
            c = cos[None, None]
            xe = x[..., ::2]
            xo = x[..., 1::2]
            re = xe * c - xo * s
            ro = xe * s + xo * c
            return jnp.stack((re, ro), axis=-1).reshape(x.shape)

        def _heads(t):
            b, n, _ = t.shape
            return t.reshape(b, n, H, DH).transpose(0, 2, 1, 3)

        def _attn(xq, ctx, wq, wkv, wo, bo):
            q = _heads(xq @ wq)
            k, v = jnp.split(ctx @ wkv, 2, axis=-1)
            k = _heads(k)
            v = _heads(v)
            sq, cq = _sincos(q.shape[2], DH)
            sk, ck = _sincos(k.shape[2], DH)
            q = _rope(q, sq, cq)
            k = _rope(k, sk, ck)
            sim = jnp.einsum('bhnd,bhmd->bhnm', q, k) * DH ** (-0.5)
            a = jax.nn.softmax(sim, axis=-1)
            o = jnp.einsum('bhnm,bhmd->bhnd', a, v)
            o = o.transpose(0, 2, 1, 3).reshape(xq.shape[0], xq.shape[1], MID)
            return o @ wo + bo

        def _adaln(x, c, lw, lb, gw, gb, bw, bb):
            g = (c @ gw + gb)[:, None, :]
            bt = (c @ bw + bb)[:, None, :]
            return _ln(x, lw, lb) * (1.0 + g) + bt
        ks = jax.random.split(jax.random.key(seed), 24)
        s = 0.02
        inp = {'x': jax.random.normal(ks[0], (B, N, D), jnp.float32), 'cond': jax.random.normal(ks[1], (B, D), jnp.float32), 'context': jax.random.normal(ks[2], (B, M, DC), jnp.float32), 'ln1_w': jnp.ones((D,), jnp.float32), 'ln1_b': jnp.zeros((D,), jnp.float32), 'g1_w': jax.random.normal(ks[3], (D, D), jnp.float32) * s, 'g1_b': jnp.zeros((D,), jnp.float32), 'b1_w': jax.random.normal(ks[4], (D, D), jnp.float32) * s, 'b1_b': jnp.zeros((D,), jnp.float32), 'ln2_w': jnp.ones((D,), jnp.float32), 'ln2_b': jnp.zeros((D,), jnp.float32), 'g2_w': jax.random.normal(ks[5], (D, D), jnp.float32) * s, 'g2_b': jnp.zeros((D,), jnp.float32), 'b2_w': jax.random.normal(ks[6], (D, D), jnp.float32) * s, 'b2_b': jnp.zeros((D,), jnp.float32), 'sa_wq': jax.random.normal(ks[7], (D, MID), jnp.float32) * s, 'sa_wkv': jax.random.normal(ks[8], (D, 2 * MID), jnp.float32) * s, 'sa_wo': jax.random.normal(ks[9], (MID, D), jnp.float32) * s, 'sa_bo': jnp.zeros((D,), jnp.float32), 'ca_lnc_w': jnp.ones((DC,), jnp.float32), 'ca_lnc_b': jnp.zeros((DC,), jnp.float32), 'ca_wq': jax.random.normal(ks[10], (D, MID), jnp.float32) * s, 'ca_wkv': jax.random.normal(ks[11], (DC, 2 * MID), jnp.float32) * s, 'ca_wo': jax.random.normal(ks[12], (MID, D), jnp.float32) * s, 'ca_bo': jnp.zeros((D,), jnp.float32), 'ff_w1': jax.random.normal(ks[13], (D, MULT * D), jnp.float32) * s, 'ff_b1': jnp.zeros((MULT * D,), jnp.float32), 'ff_w2': jax.random.normal(ks[14], (MULT * D, D), jnp.float32) * s, 'ff_b2': jnp.zeros((D,), jnp.float32)}
        return inp
    _L1_xcond_all = _L1_xcond_setup()
    _L1_xcond_in = {k: v for k, v in _L1_xcond_all.items() if k in ('ln1_w', 'ln1_b', 'g1_w', 'g1_b', 'b1_w', 'b1_b', 'ln2_w', 'ln2_b', 'g2_w', 'g2_b', 'b2_w', 'b2_b', 'sa_wq', 'sa_wkv', 'sa_wo', 'sa_bo', 'ca_lnc_w', 'ca_lnc_b', 'ca_wq', 'ca_wkv', 'ca_wo', 'ca_bo', 'ff_w1', 'ff_b1', 'ff_w2', 'ff_b2')}
    del _L1_xcond_all

    def _L2_xcond_setup():
        import jax, jax.numpy as jnp
        import numpy as np
        EPS = 1e-05

        def _ada_ln(x, t, W, b):
            emb = t @ W + b
            scale, shift = jnp.split(emb, 2, axis=-1)
            mu = x.mean(-1, keepdims=True)
            var = ((x - mu) ** 2).mean(-1, keepdims=True)
            xn = (x - mu) * jax.lax.rsqrt(var + EPS)
            return xn * (1.0 + scale) + shift

        def _attn(x, ctx, Wq, Wk, Wv, Wo, bo, heads):
            b, n, _ = x.shape
            j = ctx.shape[1]
            q = (x @ Wq).reshape(b, n, heads, -1)
            k = (ctx @ Wk).reshape(b, j, heads, -1)
            v = (ctx @ Wv).reshape(b, j, heads, -1)
            scale = q.shape[-1] ** (-0.5)
            sim = jnp.einsum('bihd,bjhd->bhij', q, k) * scale
            attn = jax.nn.softmax(sim, axis=-1)
            out = jnp.einsum('bhij,bjhd->bihd', attn, v).reshape(b, n, -1)
            return out @ Wo + bo

        def _ff(x, W1, b1, W2, b2):
            p = x @ W1 + b1
            a, gate = jnp.split(p, 2, axis=-1)
            return a * jax.nn.gelu(gate, approximate=False) @ W2 + b2
        key = jax.random.key(seed)
        ks = jax.random.split(key, 32)
        B, N, D = (4, 256, 128)
        J, CD = (32, 96)
        H, DH = (16, 64)
        INNER = H * DH
        FF = 4 * D
        w = lambda k, shp: jax.random.normal(k, shp, jnp.float32) * 0.02
        inp = {'x': jax.random.normal(ks[0], (B, N, D), jnp.float32), 't': jax.random.normal(ks[1], (B, 1, D), jnp.float32), 'context': jax.random.normal(ks[2], (B, J, CD), jnp.float32), 'n1_w': w(ks[3], (D, 2 * D)), 'n1_b': jnp.zeros((2 * D,), jnp.float32), 'n2_w': w(ks[4], (D, 2 * D)), 'n2_b': jnp.zeros((2 * D,), jnp.float32), 'n3_w': w(ks[5], (D, 2 * D)), 'n3_b': jnp.zeros((2 * D,), jnp.float32), 'q1': w(ks[6], (D, INNER)), 'k1': w(ks[7], (D, INNER)), 'v1': w(ks[8], (D, INNER)), 'o1_w': w(ks[9], (INNER, D)), 'o1_b': jnp.zeros((D,), jnp.float32), 'q2': w(ks[10], (D, INNER)), 'k2': w(ks[11], (CD, INNER)), 'v2': w(ks[12], (CD, INNER)), 'o2_w': w(ks[13], (INNER, D)), 'o2_b': jnp.zeros((D,), jnp.float32), 'ff_w1': w(ks[14], (D, 2 * FF)), 'ff_b1': jnp.zeros((2 * FF,), jnp.float32), 'ff_w2': w(ks[15], (FF, D)), 'ff_b2': jnp.zeros((D,), jnp.float32)}
        return inp
    _L2_xcond_all = _L2_xcond_setup()
    _L2_xcond_in = {k: v for k, v in _L2_xcond_all.items() if k in ('n1_w', 'n1_b', 'n2_w', 'n2_b', 'n3_w', 'n3_b', 'q1', 'k1', 'v1', 'o1_w', 'o1_b', 'q2', 'k2', 'v2', 'o2_w', 'o2_b', 'ff_w1', 'ff_b1', 'ff_w2', 'ff_b2')}
    del _L2_xcond_all

    def _L3_xcond_setup():
        import jax, jax.numpy as jnp
        import numpy as np
        B, N, D, H, TD, TL = (4, 128, 128, 16, 96, 77)
        HD = D // H
        EPS = 1e-06

        def _ln(x):
            mu = jnp.mean(x, axis=-1, keepdims=True)
            var = jnp.var(x, axis=-1, keepdims=True)
            return (x - mu) * jax.lax.rsqrt(var + EPS)

        def _modulate(x, shift, scale):
            return x * (1.0 + scale[:, None, :]) + shift[:, None, :]

        def _heads(t):
            return t.reshape(t.shape[0], t.shape[1], H, HD).transpose(0, 2, 1, 3)

        def _attend(q, k, v):
            sim = jnp.einsum('bhid,bhjd->bhij', q, k) * HD ** (-0.5)
            attn = jax.nn.softmax(sim, axis=-1)
            out = jnp.einsum('bhij,bhjd->bhid', attn, v)
            return out.transpose(0, 2, 1, 3).reshape(out.shape[0], -1, D)
        key = jax.random.key(seed)
        ks = jax.random.split(key, 16)
        s = 0.02
        return {'x': jax.random.normal(ks[0], (B, N, D), jnp.float32), 'c': jax.random.normal(ks[1], (B, D), jnp.float32), 'text_embed': jax.random.normal(ks[2], (B, TL, TD), jnp.float32), 'W_ada': jax.random.normal(ks[3], (D, 6 * D), jnp.float32) * s, 'b_ada': jnp.zeros((6 * D,), jnp.float32), 'W_qkv': jax.random.normal(ks[4], (D, 3 * D), jnp.float32) * s, 'b_qkv': jnp.zeros((3 * D,), jnp.float32), 'W_proj': jax.random.normal(ks[5], (D, D), jnp.float32) * s, 'b_proj': jnp.zeros((D,), jnp.float32), 'W_ctx': jax.random.normal(ks[6], (TD, D), jnp.float32) * s, 'b_ctx': jnp.zeros((D,), jnp.float32), 'W_q': jax.random.normal(ks[7], (D, D), jnp.float32) * s, 'W_k': jax.random.normal(ks[8], (D, D), jnp.float32) * s, 'W_v': jax.random.normal(ks[9], (D, D), jnp.float32) * s, 'W_out': jax.random.normal(ks[10], (D, D), jnp.float32) * s, 'b_out': jnp.zeros((D,), jnp.float32), 'W_fc1': jax.random.normal(ks[11], (D, 4 * D), jnp.float32) * s, 'b_fc1': jnp.zeros((4 * D,), jnp.float32), 'W_fc2': jax.random.normal(ks[12], (4 * D, D), jnp.float32) * s, 'b_fc2': jnp.zeros((D,), jnp.float32)}
    _L3_xcond_all = _L3_xcond_setup()
    _L3_xcond_in = {k: v for k, v in _L3_xcond_all.items() if k in ('W_ada', 'b_ada', 'W_qkv', 'b_qkv', 'W_proj', 'b_proj', 'W_ctx', 'b_ctx', 'W_q', 'W_k', 'W_v', 'W_out', 'b_out', 'W_fc1', 'b_fc1', 'W_fc2', 'b_fc2')}
    del _L3_xcond_all
    return {'x': x, 'ctx_768': ctx_768, 'cond_1024': cond_1024, 'L0_xcond_ln1_w': _L0_xcond_in['ln1_w'], 'L0_xcond_ln1_b': _L0_xcond_in['ln1_b'], 'L0_xcond_ln2_w': _L0_xcond_in['ln2_w'], 'L0_xcond_ln2_b': _L0_xcond_in['ln2_b'], 'L0_xcond_ln3_w': _L0_xcond_in['ln3_w'], 'L0_xcond_ln3_b': _L0_xcond_in['ln3_b'], 'L0_xcond_Wqkv': _L0_xcond_in['Wqkv'], 'L0_xcond_bqkv': _L0_xcond_in['bqkv'], 'L0_xcond_Wos': _L0_xcond_in['Wos'], 'L0_xcond_bos': _L0_xcond_in['bos'], 'L0_xcond_Wq': _L0_xcond_in['Wq'], 'L0_xcond_bq': _L0_xcond_in['bq'], 'L0_xcond_Wk': _L0_xcond_in['Wk'], 'L0_xcond_bk': _L0_xcond_in['bk'], 'L0_xcond_Wv': _L0_xcond_in['Wv'], 'L0_xcond_bv': _L0_xcond_in['bv'], 'L0_xcond_Woc': _L0_xcond_in['Woc'], 'L0_xcond_boc': _L0_xcond_in['boc'], 'L0_xcond_W1': _L0_xcond_in['W1'], 'L0_xcond_b1': _L0_xcond_in['b1'], 'L0_xcond_W2': _L0_xcond_in['W2'], 'L0_xcond_b2': _L0_xcond_in['b2'], 'L0_xcond_Wmod': _L0_xcond_in['Wmod'], 'L0_xcond_bmod': _L0_xcond_in['bmod'], 'L1_xcond_ln1_w': _L1_xcond_in['ln1_w'], 'L1_xcond_ln1_b': _L1_xcond_in['ln1_b'], 'L1_xcond_g1_w': _L1_xcond_in['g1_w'], 'L1_xcond_g1_b': _L1_xcond_in['g1_b'], 'L1_xcond_b1_w': _L1_xcond_in['b1_w'], 'L1_xcond_b1_b': _L1_xcond_in['b1_b'], 'L1_xcond_ln2_w': _L1_xcond_in['ln2_w'], 'L1_xcond_ln2_b': _L1_xcond_in['ln2_b'], 'L1_xcond_g2_w': _L1_xcond_in['g2_w'], 'L1_xcond_g2_b': _L1_xcond_in['g2_b'], 'L1_xcond_b2_w': _L1_xcond_in['b2_w'], 'L1_xcond_b2_b': _L1_xcond_in['b2_b'], 'L1_xcond_sa_wq': _L1_xcond_in['sa_wq'], 'L1_xcond_sa_wkv': _L1_xcond_in['sa_wkv'], 'L1_xcond_sa_wo': _L1_xcond_in['sa_wo'], 'L1_xcond_sa_bo': _L1_xcond_in['sa_bo'], 'L1_xcond_ca_lnc_w': _L1_xcond_in['ca_lnc_w'], 'L1_xcond_ca_lnc_b': _L1_xcond_in['ca_lnc_b'], 'L1_xcond_ca_wq': _L1_xcond_in['ca_wq'], 'L1_xcond_ca_wkv': _L1_xcond_in['ca_wkv'], 'L1_xcond_ca_wo': _L1_xcond_in['ca_wo'], 'L1_xcond_ca_bo': _L1_xcond_in['ca_bo'], 'L1_xcond_ff_w1': _L1_xcond_in['ff_w1'], 'L1_xcond_ff_b1': _L1_xcond_in['ff_b1'], 'L1_xcond_ff_w2': _L1_xcond_in['ff_w2'], 'L1_xcond_ff_b2': _L1_xcond_in['ff_b2'], 'L2_xcond_n1_w': _L2_xcond_in['n1_w'], 'L2_xcond_n1_b': _L2_xcond_in['n1_b'], 'L2_xcond_n2_w': _L2_xcond_in['n2_w'], 'L2_xcond_n2_b': _L2_xcond_in['n2_b'], 'L2_xcond_n3_w': _L2_xcond_in['n3_w'], 'L2_xcond_n3_b': _L2_xcond_in['n3_b'], 'L2_xcond_q1': _L2_xcond_in['q1'], 'L2_xcond_k1': _L2_xcond_in['k1'], 'L2_xcond_v1': _L2_xcond_in['v1'], 'L2_xcond_o1_w': _L2_xcond_in['o1_w'], 'L2_xcond_o1_b': _L2_xcond_in['o1_b'], 'L2_xcond_q2': _L2_xcond_in['q2'], 'L2_xcond_k2': _L2_xcond_in['k2'], 'L2_xcond_v2': _L2_xcond_in['v2'], 'L2_xcond_o2_w': _L2_xcond_in['o2_w'], 'L2_xcond_o2_b': _L2_xcond_in['o2_b'], 'L2_xcond_ff_w1': _L2_xcond_in['ff_w1'], 'L2_xcond_ff_b1': _L2_xcond_in['ff_b1'], 'L2_xcond_ff_w2': _L2_xcond_in['ff_w2'], 'L2_xcond_ff_b2': _L2_xcond_in['ff_b2'], 'L3_xcond_W_ada': _L3_xcond_in['W_ada'], 'L3_xcond_b_ada': _L3_xcond_in['b_ada'], 'L3_xcond_W_qkv': _L3_xcond_in['W_qkv'], 'L3_xcond_b_qkv': _L3_xcond_in['b_qkv'], 'L3_xcond_W_proj': _L3_xcond_in['W_proj'], 'L3_xcond_b_proj': _L3_xcond_in['b_proj'], 'L3_xcond_W_ctx': _L3_xcond_in['W_ctx'], 'L3_xcond_b_ctx': _L3_xcond_in['b_ctx'], 'L3_xcond_W_q': _L3_xcond_in['W_q'], 'L3_xcond_W_k': _L3_xcond_in['W_k'], 'L3_xcond_W_v': _L3_xcond_in['W_v'], 'L3_xcond_W_out': _L3_xcond_in['W_out'], 'L3_xcond_b_out': _L3_xcond_in['b_out'], 'L3_xcond_W_fc1': _L3_xcond_in['W_fc1'], 'L3_xcond_b_fc1': _L3_xcond_in['b_fc1'], 'L3_xcond_W_fc2': _L3_xcond_in['W_fc2'], 'L3_xcond_b_fc2': _L3_xcond_in['b_fc2']}

def reference(x, ctx_768, cond_1024, L0_xcond_ln1_w, L0_xcond_ln1_b, L0_xcond_ln2_w, L0_xcond_ln2_b, L0_xcond_ln3_w, L0_xcond_ln3_b, L0_xcond_Wqkv, L0_xcond_bqkv, L0_xcond_Wos, L0_xcond_bos, L0_xcond_Wq, L0_xcond_bq, L0_xcond_Wk, L0_xcond_bk, L0_xcond_Wv, L0_xcond_bv, L0_xcond_Woc, L0_xcond_boc, L0_xcond_W1, L0_xcond_b1, L0_xcond_W2, L0_xcond_b2, L0_xcond_Wmod, L0_xcond_bmod, L1_xcond_ln1_w, L1_xcond_ln1_b, L1_xcond_g1_w, L1_xcond_g1_b, L1_xcond_b1_w, L1_xcond_b1_b, L1_xcond_ln2_w, L1_xcond_ln2_b, L1_xcond_g2_w, L1_xcond_g2_b, L1_xcond_b2_w, L1_xcond_b2_b, L1_xcond_sa_wq, L1_xcond_sa_wkv, L1_xcond_sa_wo, L1_xcond_sa_bo, L1_xcond_ca_lnc_w, L1_xcond_ca_lnc_b, L1_xcond_ca_wq, L1_xcond_ca_wkv, L1_xcond_ca_wo, L1_xcond_ca_bo, L1_xcond_ff_w1, L1_xcond_ff_b1, L1_xcond_ff_w2, L1_xcond_ff_b2, L2_xcond_n1_w, L2_xcond_n1_b, L2_xcond_n2_w, L2_xcond_n2_b, L2_xcond_n3_w, L2_xcond_n3_b, L2_xcond_q1, L2_xcond_k1, L2_xcond_v1, L2_xcond_o1_w, L2_xcond_o1_b, L2_xcond_q2, L2_xcond_k2, L2_xcond_v2, L2_xcond_o2_w, L2_xcond_o2_b, L2_xcond_ff_w1, L2_xcond_ff_b1, L2_xcond_ff_w2, L2_xcond_ff_b2, L3_xcond_W_ada, L3_xcond_b_ada, L3_xcond_W_qkv, L3_xcond_b_qkv, L3_xcond_W_proj, L3_xcond_b_proj, L3_xcond_W_ctx, L3_xcond_b_ctx, L3_xcond_W_q, L3_xcond_W_k, L3_xcond_W_v, L3_xcond_W_out, L3_xcond_b_out, L3_xcond_W_fc1, L3_xcond_b_fc1, L3_xcond_W_fc2, L3_xcond_b_fc2):
    import jax
    import jax.numpy as jnp

    def _L0_xcond_ref(x, context, time_emb, ln1_w, ln1_b, ln2_w, ln2_b, ln3_w, ln3_b, Wqkv, bqkv, Wos, bos, Wq, bq, Wk, bk, Wv, bv, Woc, boc, W1, b1, W2, b2, Wmod, bmod):
        import jax, jax.numpy as jnp
        import numpy as np
        D = 128
        CD = 96
        H = 16
        HD = D // H
        EPS = 1e-05

        def _ln(x, w, b):
            m = jnp.mean(x, axis=-1, keepdims=True)
            v = jnp.var(x, axis=-1, keepdims=True)
            return (x - m) * jax.lax.rsqrt(v + EPS) * w + b

        def _attn(q, k, v):
            q = q.reshape(q.shape[0], q.shape[1], H, HD).transpose(0, 2, 1, 3)
            k = k.reshape(k.shape[0], k.shape[1], H, HD).transpose(0, 2, 1, 3)
            v = v.reshape(v.shape[0], v.shape[1], H, HD).transpose(0, 2, 1, 3)
            scores = jnp.einsum('bhnd,bhmd->bhnm', q, k) * HD ** (-0.5)
            p = jax.nn.softmax(scores, axis=-1)
            o = jnp.einsum('bhnm,bhmd->bhnd', p, v)
            return o.transpose(0, 2, 1, 3).reshape(o.shape[0], o.shape[2], D)
        mod = jax.nn.silu(time_emb) @ Wmod + bmod
        sh1, sc1, sh2, sc2, sh3, sc3 = jnp.split(mod, 6, axis=-1)
        h = _ln(x, ln1_w, ln1_b) * (1 + sc1[:, None, :]) + sh1[:, None, :]
        qkv = h @ Wqkv + bqkv
        q, k, v = jnp.split(qkv, 3, axis=-1)
        x = x + _attn(q, k, v) @ Wos + bos
        h = _ln(x, ln2_w, ln2_b) * (1 + sc2[:, None, :]) + sh2[:, None, :]
        x = x + _attn(h @ Wq + bq, context @ Wk + bk, context @ Wv + bv) @ Woc + boc
        h = _ln(x, ln3_w, ln3_b) * (1 + sc3[:, None, :]) + sh3[:, None, :]
        x = x + jax.nn.gelu(h @ W1 + b1, approximate=False) @ W2 + b2
        return x

    def _L1_xcond_ref(x, cond, context, ln1_w, ln1_b, g1_w, g1_b, b1_w, b1_b, ln2_w, ln2_b, g2_w, g2_b, b2_w, b2_b, sa_wq, sa_wkv, sa_wo, sa_bo, ca_lnc_w, ca_lnc_b, ca_wq, ca_wkv, ca_wo, ca_bo, ff_w1, ff_b1, ff_w2, ff_b2):
        import jax, jax.numpy as jnp
        import numpy as np
        B, N, M = (2, 128, 64)
        D, H, DH = (128, 16, 64)
        MID = H * DH
        DC = 96
        MULT = 4
        EPS = 1e-05

        def _ln(x, w, b):
            mu = jnp.mean(x, -1, keepdims=True)
            var = jnp.mean((x - mu) ** 2, -1, keepdims=True)
            return (x - mu) * jax.lax.rsqrt(var + EPS) * w + b

        def _sincos(n, d):
            inv = 1.0 / 10000.0 ** (jnp.arange(0, d, 2, dtype=jnp.float32) / d)
            ang = jnp.arange(n, dtype=jnp.float32)[:, None] * inv[None, :]
            return (jnp.sin(ang), jnp.cos(ang))

        def _rope(x, sin, cos):
            s = sin[None, None]
            c = cos[None, None]
            xe = x[..., ::2]
            xo = x[..., 1::2]
            re = xe * c - xo * s
            ro = xe * s + xo * c
            return jnp.stack((re, ro), axis=-1).reshape(x.shape)

        def _heads(t):
            b, n, _ = t.shape
            return t.reshape(b, n, H, DH).transpose(0, 2, 1, 3)

        def _attn(xq, ctx, wq, wkv, wo, bo):
            q = _heads(xq @ wq)
            k, v = jnp.split(ctx @ wkv, 2, axis=-1)
            k = _heads(k)
            v = _heads(v)
            sq, cq = _sincos(q.shape[2], DH)
            sk, ck = _sincos(k.shape[2], DH)
            q = _rope(q, sq, cq)
            k = _rope(k, sk, ck)
            sim = jnp.einsum('bhnd,bhmd->bhnm', q, k) * DH ** (-0.5)
            a = jax.nn.softmax(sim, axis=-1)
            o = jnp.einsum('bhnm,bhmd->bhnd', a, v)
            o = o.transpose(0, 2, 1, 3).reshape(xq.shape[0], xq.shape[1], MID)
            return o @ wo + bo

        def _adaln(x, c, lw, lb, gw, gb, bw, bb):
            g = (c @ gw + gb)[:, None, :]
            bt = (c @ bw + bb)[:, None, :]
            return _ln(x, lw, lb) * (1.0 + g) + bt
        attn_in = _adaln(x, cond, ln1_w, ln1_b, g1_w, g1_b, b1_w, b1_b)
        x = _attn(attn_in, attn_in, sa_wq, sa_wkv, sa_wo, sa_bo) + x
        cross_in = _adaln(x, cond, ln1_w, ln1_b, g1_w, g1_b, b1_w, b1_b)
        ctx_n = _ln(context, ca_lnc_w, ca_lnc_b)
        x = _attn(cross_in, ctx_n, ca_wq, ca_wkv, ca_wo, ca_bo) + x
        ffn_in = _adaln(x, cond, ln2_w, ln2_b, g2_w, g2_b, b2_w, b2_b)
        h = jax.nn.gelu(ffn_in @ ff_w1 + ff_b1, approximate=False)
        x = h @ ff_w2 + ff_b2 + x
        return x

    def _L2_xcond_ref(x, t, context, n1_w, n1_b, n2_w, n2_b, n3_w, n3_b, q1, k1, v1, o1_w, o1_b, q2, k2, v2, o2_w, o2_b, ff_w1, ff_b1, ff_w2, ff_b2):
        import jax, jax.numpy as jnp
        import numpy as np
        EPS = 1e-05

        def _ada_ln(x, t, W, b):
            emb = t @ W + b
            scale, shift = jnp.split(emb, 2, axis=-1)
            mu = x.mean(-1, keepdims=True)
            var = ((x - mu) ** 2).mean(-1, keepdims=True)
            xn = (x - mu) * jax.lax.rsqrt(var + EPS)
            return xn * (1.0 + scale) + shift

        def _attn(x, ctx, Wq, Wk, Wv, Wo, bo, heads):
            b, n, _ = x.shape
            j = ctx.shape[1]
            q = (x @ Wq).reshape(b, n, heads, -1)
            k = (ctx @ Wk).reshape(b, j, heads, -1)
            v = (ctx @ Wv).reshape(b, j, heads, -1)
            scale = q.shape[-1] ** (-0.5)
            sim = jnp.einsum('bihd,bjhd->bhij', q, k) * scale
            attn = jax.nn.softmax(sim, axis=-1)
            out = jnp.einsum('bhij,bjhd->bihd', attn, v).reshape(b, n, -1)
            return out @ Wo + bo

        def _ff(x, W1, b1, W2, b2):
            p = x @ W1 + b1
            a, gate = jnp.split(p, 2, axis=-1)
            return a * jax.nn.gelu(gate, approximate=False) @ W2 + b2
        H = 16
        h = _ada_ln(x, t, n1_w, n1_b)
        x = _attn(h, h, q1, k1, v1, o1_w, o1_b, H) + x
        h = _ada_ln(x, t, n2_w, n2_b)
        x = _attn(h, context, q2, k2, v2, o2_w, o2_b, H) + x
        h = _ada_ln(x, t, n3_w, n3_b)
        x = _ff(h, ff_w1, ff_b1, ff_w2, ff_b2) + x
        return x

    def _L3_xcond_ref(x, c, text_embed, W_ada, b_ada, W_qkv, b_qkv, W_proj, b_proj, W_ctx, b_ctx, W_q, W_k, W_v, W_out, b_out, W_fc1, b_fc1, W_fc2, b_fc2):
        import jax, jax.numpy as jnp
        import numpy as np
        B, N, D, H, TD, TL = (4, 128, 128, 16, 96, 77)
        HD = D // H
        EPS = 1e-06

        def _ln(x):
            mu = jnp.mean(x, axis=-1, keepdims=True)
            var = jnp.var(x, axis=-1, keepdims=True)
            return (x - mu) * jax.lax.rsqrt(var + EPS)

        def _modulate(x, shift, scale):
            return x * (1.0 + scale[:, None, :]) + shift[:, None, :]

        def _heads(t):
            return t.reshape(t.shape[0], t.shape[1], H, HD).transpose(0, 2, 1, 3)

        def _attend(q, k, v):
            sim = jnp.einsum('bhid,bhjd->bhij', q, k) * HD ** (-0.5)
            attn = jax.nn.softmax(sim, axis=-1)
            out = jnp.einsum('bhij,bhjd->bhid', attn, v)
            return out.transpose(0, 2, 1, 3).reshape(out.shape[0], -1, D)
        mod = jax.nn.silu(c) @ W_ada + b_ada
        sh_msa, sc_msa, sh_x, sc_x, sh_mlp, sc_mlp = jnp.split(mod, 6, axis=-1)
        h1 = _modulate(_ln(x), sh_msa, sc_msa)
        qkv = h1 @ W_qkv + b_qkv
        q, k, v = jnp.split(qkv, 3, axis=-1)
        out = _attend(_heads(q), _heads(k), _heads(v))
        x = x + (out @ W_proj + b_proj)
        h2 = _modulate(_ln(x), sh_x, sc_x)
        ctx = text_embed @ W_ctx + b_ctx
        q = _heads(h2 @ W_q)
        k = _heads(ctx @ W_k)
        v = _heads(ctx @ W_v)
        out = _attend(q, k, v)
        x = x + (out @ W_out + b_out)
        h3 = _modulate(_ln(x), sh_mlp, sc_mlp)
        hidden = jax.nn.gelu(h3 @ W_fc1 + b_fc1, approximate=True)
        x = x + (hidden @ W_fc2 + b_fc2)
        return x
    x = _L0_xcond_ref(x, ctx_768, cond_1024, L0_xcond_ln1_w, L0_xcond_ln1_b, L0_xcond_ln2_w, L0_xcond_ln2_b, L0_xcond_ln3_w, L0_xcond_ln3_b, L0_xcond_Wqkv, L0_xcond_bqkv, L0_xcond_Wos, L0_xcond_bos, L0_xcond_Wq, L0_xcond_bq, L0_xcond_Wk, L0_xcond_bk, L0_xcond_Wv, L0_xcond_bv, L0_xcond_Woc, L0_xcond_boc, L0_xcond_W1, L0_xcond_b1, L0_xcond_W2, L0_xcond_b2, L0_xcond_Wmod, L0_xcond_bmod)
    x = _L1_xcond_ref(x, cond_1024, ctx_768, L1_xcond_ln1_w, L1_xcond_ln1_b, L1_xcond_g1_w, L1_xcond_g1_b, L1_xcond_b1_w, L1_xcond_b1_b, L1_xcond_ln2_w, L1_xcond_ln2_b, L1_xcond_g2_w, L1_xcond_g2_b, L1_xcond_b2_w, L1_xcond_b2_b, L1_xcond_sa_wq, L1_xcond_sa_wkv, L1_xcond_sa_wo, L1_xcond_sa_bo, L1_xcond_ca_lnc_w, L1_xcond_ca_lnc_b, L1_xcond_ca_wq, L1_xcond_ca_wkv, L1_xcond_ca_wo, L1_xcond_ca_bo, L1_xcond_ff_w1, L1_xcond_ff_b1, L1_xcond_ff_w2, L1_xcond_ff_b2)
    x = _L2_xcond_ref(x, cond_1024[:, None, :], ctx_768, L2_xcond_n1_w, L2_xcond_n1_b, L2_xcond_n2_w, L2_xcond_n2_b, L2_xcond_n3_w, L2_xcond_n3_b, L2_xcond_q1, L2_xcond_k1, L2_xcond_v1, L2_xcond_o1_w, L2_xcond_o1_b, L2_xcond_q2, L2_xcond_k2, L2_xcond_v2, L2_xcond_o2_w, L2_xcond_o2_b, L2_xcond_ff_w1, L2_xcond_ff_b1, L2_xcond_ff_w2, L2_xcond_ff_b2)
    x = _L3_xcond_ref(x, cond_1024, ctx_768, L3_xcond_W_ada, L3_xcond_b_ada, L3_xcond_W_qkv, L3_xcond_b_qkv, L3_xcond_W_proj, L3_xcond_b_proj, L3_xcond_W_ctx, L3_xcond_b_ctx, L3_xcond_W_q, L3_xcond_W_k, L3_xcond_W_v, L3_xcond_W_out, L3_xcond_b_out, L3_xcond_W_fc1, L3_xcond_b_fc1, L3_xcond_W_fc2, L3_xcond_b_fc2)
    return x

_drawn_inputs = setup_inputs


def setup_inputs(seed=0):
    import zlib

    import numpy as np

    out = dict(_drawn_inputs(seed))
    spreads = {'L0_xcond_ln1_w': (1.0, 0.6),
     'L0_xcond_ln1_b': (0.0, 0.8),
     'L0_xcond_ln2_w': (1.0, 0.6),
     'L0_xcond_ln2_b': (0.0, 0.8),
     'L0_xcond_ln3_w': (1.0, 0.6),
     'L0_xcond_ln3_b': (0.0, 0.8),
     'L0_xcond_bqkv': (0.0, 0.345),
     'L0_xcond_bos': (0.0, 0.1),
     'L0_xcond_bq': (0.0, 2.0),
     'L0_xcond_bk': (0.0, 2.0),
     'L0_xcond_bv': (0.0, 0.402),
     'L0_xcond_boc': (0.0, 0.1),
     'L0_xcond_b1': (0.0, 0.333),
     'L0_xcond_b2': (0.0, 0.1),
     'L0_xcond_bmod': (0.0, 0.8),
     'L1_xcond_ln1_w': (1.0, 0.6),
     'L1_xcond_ln1_b': (0.0, 0.489),
     'L1_xcond_g1_b': (0.0, 0.8),
     'L1_xcond_b1_b': (0.0, 0.597),
     'L1_xcond_ln2_w': (1.0, 0.6),
     'L1_xcond_ln2_b': (0.0, 0.8),
     'L1_xcond_g2_b': (0.0, 0.8),
     'L1_xcond_b2_b': (0.0, 0.8),
     'L1_xcond_sa_bo': (0.0, 0.1),
     'L1_xcond_ca_lnc_w': (1.0, 0.6),
     'L1_xcond_ca_lnc_b': (0.0, 0.682),
     'L1_xcond_ca_bo': (0.0, 0.1),
     'L1_xcond_ff_b1': (0.0, 0.341),
     'L1_xcond_ff_b2': (0.0, 0.1),
     'L2_xcond_n1_b': (0.0, 0.624),
     'L2_xcond_n2_b': (0.0, 0.8),
     'L2_xcond_n3_b': (0.0, 0.8),
     'L2_xcond_o1_b': (0.0, 0.1),
     'L2_xcond_o2_b': (0.0, 0.1),
     'L2_xcond_ff_b1': (0.0, 0.8),
     'L2_xcond_ff_b2': (0.0, 0.527),
     'L3_xcond_b_ada': (0.0, 0.8),
     'L3_xcond_b_qkv': (0.0, 2.0),
     'L3_xcond_b_proj': (0.0, 0.525),
     'L3_xcond_b_ctx': (0.0, 0.8),
     'L3_xcond_b_out': (0.0, 0.8),
     'L3_xcond_b_fc1': (0.0, 2.0),
     'L3_xcond_b_fc2': (0.0, 0.8)}
    factors = {'L0_xcond_Wqkv': 5.063,
     'L0_xcond_Wq': 8.0,
     'L0_xcond_Wk': 8.0,
     'L0_xcond_Wmod': 4.536,
     'L1_xcond_g1_w': 8.0,
     'L1_xcond_g2_w': 4.911,
     'L1_xcond_b2_w': 4.983,
     'L1_xcond_sa_wq': 8.0,
     'L1_xcond_ca_wq': 8.0,
     'L2_xcond_n2_w': 8.0,
     'L2_xcond_n3_w': 8.0,
     'L2_xcond_q1': 8.0,
     'L2_xcond_k1': 8.0,
     'L2_xcond_q2': 8.0,
     'L2_xcond_k2': 8.0,
     'L2_xcond_ff_w1': 3.737,
     'L2_xcond_ff_w2': 3.693,
     'L3_xcond_W_ada': 4.527,
     'L3_xcond_W_qkv': 3.2,
     'L3_xcond_W_ctx': 8.0,
     'L3_xcond_W_q': 8.0,
     'L3_xcond_W_k': 8.0,
     'L3_xcond_W_v': 8.0,
     'L3_xcond_W_out': 8.0,
     'L3_xcond_W_fc1': 5.799,
     'L3_xcond_W_fc2': 4.254}
    for name, (base, spread) in spreads.items():
        noise = np.random.default_rng([zlib.crc32(name.encode()), seed]).standard_normal(out[name].shape)
        drawn = base * np.exp(spread * noise) if base else spread * noise
        out[name] = jnp.asarray(drawn.astype(out[name].dtype))
    for name, factor in factors.items():
        out[name] = (out[name] * factor).astype(out[name].dtype)
    return out
```

```python
from contextlib import ExitStack

import concourse.bass as bass
from concourse import mybir

ALU = mybir.AluOpType
ACT = mybir.ActivationFunctionType
AX = mybir.AxisListType
F32 = mybir.dt.float32

P = 128
B = 8
NB = 2
TURNS = B // NB
W = NB * P
CD = 96
H = 16
G = 8
J = 2 * NB
LAYERS = 4
SUBS = 3 * LAYERS
ATT = 2 * LAYERS
F = 4
HALF = 64

HEAD = [8, 64, 64, 8]
ROPE = [False, True, False, False]
GLU = [False, False, True, False]
EPS = [1e-5, 1e-5, 1e-5, 1e-6]
GELU = [ACT.Gelu, ACT.Gelu, ACT.Gelu, ACT.Gelu_apprx_tanh]
QK_BIAS = [(True, True), (False, False), (False, False), (True, False)]


def weight_columns(s):
    layer, kind = divmod(s, 3)
    if kind == 2:
        parts = [("w1", F * P * (2 if GLU[layer] else 1)), ("w2", F * P)]
    else:
        narrow = HEAD[layer] == 8
        parts = [("q", G * P), ("k", G * P), ("v", H * HEAD[layer]), ("o", P if narrow else G * P)]
        if ROPE[layer]:
            parts += [("q_swapped", G * P), ("k_swapped", G * P)]
    at, where = 0, {}
    for name, width in parts:
        where[name] = (at, width)
        at += width
    return where, at


def small_columns():
    parts = [("ident", P), ("cond", B), ("mod_b", 2 * SUBS), ("ln_w", SUBS), ("ln_b", SUBS),
             ("ctx_w", P), ("ctx_b", 1), ("ctx_ln_w", 1), ("ctx_ln_b", 1), ("cos", P), ("sin", P),
             ("qk_b", ATT * 2 * G), ("v_b", ATT * P), ("out_b", SUBS * P), ("h_b", LAYERS * 2 * F)]
    at, where = 0, {}
    for name, width in parts:
        where[name] = (at, width)
        at += width
    return where, at


def build(nc, x, ctx, small, mod_weights, weights, out):
    s_at, s_width = small_columns()
    w_at = [weight_columns(s) for s in range(SUBS)]

    with ExitStack() as stack:
        def sb(name, shape):
            return stack.enter_context(nc.sbuf_tensor(name, shape, F32))

        def sem(name):
            return stack.enter_context(nc.semaphore(name))

        sm = sb("small_sb", [P, s_width])
        w_sb = [sb(f"w_sb{s}", [P, w_at[s][1]]) for s in range(SUBS)]

        def small_part(name):
            a, n = s_at[name]
            return sm[:, a:a + n]

        def weight(s, name):
            a, n = w_at[s][0][name]
            return w_sb[s][:, a:a + n]

        ident = small_part("ident")
        MOD_HOME = 3
        mod_w = w_sb[MOD_HOME][:, 0:2 * SUBS * P]
        cond_silu = sb("cond_silu", [P, B])
        mod_sum = sb("mod_sum", [P, SUBS, 2, B])
        mod_gain = sb("mod_gain", [P, SUBS, B])
        mod_shift = sb("mod_shift", [P, SUBS, B])
        mods = sb("mods", [P, B, SUBS, 2])
        mod = sb("mod", [P, NB, SUBS, 2])
        minus_half = sb("minus_half", [P, NB])
        epsilon = sb("epsilon", [P, 2 * NB])
        wait_taker = sb("wait_taker", [P, 1])
        x_in = sb("x_in", [P, NB, P])
        ctx_in = sb("ctx_in", [P, NB, CD])
        xs = sb("xs", [P, NB, P])
        x_biased = sb("x_biased", [P, NB, P])
        x_out = sb("x_out", [P, NB, P])
        stats = sb("stats", [P, NB, 6])
        mean_var = sb("mean_var", [P, NB, 2])
        var_eps = sb("var_eps", [P, NB])
        rstd = sb("rstd", [P, NB])
        normed = sb("normed", [P, NB, P])
        hT = sb("hT", [P, W])
        ctxT = sb("ctxT", [CD, W])
        ctx_normT = sb("ctx_normT", [CD, W])
        ctx_projT = sb("ctx_projT", [P, W])
        qk = sb("qk", [P, 2, 2 * W])
        rot_a = sb("rot_a", [P, 2 * W])
        rot_b = sb("rot_b", [P, 2 * W])
        v64 = sb("v64", [P, NB, H, 65])
        v8 = sb("v8", [P, NB, H, 9])
        top = sb("top", [P, 2, J])
        shifted = sb("shifted", [P, 2, J, P])
        probsT = sb("probsT", [P, 2, J, P])
        inv = sb("inv", [P, 2, J])
        o64 = sb("o64", [P, 2, NB, P])
        o8 = sb("o8", [P, NB, P])
        oT = sb("oT", [P, G, NB, P])
        gate = sb("gate", [P, 2, W])
        hidden = sb("hidden", [P, F, W])

        ps = stack.enter_context(nc.psum_tensor("ps", [P, 8, 512], F32))
        PROJ, BACK, SCORE, TURNED, OUT = 0, 1, 2, 6, 7

        small_loaded = sem("small_loaded")
        mod_w_loaded = sem("mod_w_loaded")
        weights_loaded = [sem(f"weights_loaded{s}") for s in range(SUBS)]
        inputs_loaded = sem("inputs_loaded")
        inputs_taken = sem("inputs_taken")
        ctx_taken = sem("ctx_taken")
        consts_ready = sem("consts_ready")
        silu_ready = sem("silu_ready")
        mod_projected = sem("mod_projected")
        mod_step = sem("mod_step")
        mod_ready = sem("mod_ready")
        x_ready = sem("x_ready")
        stats_ready = sem("stats_ready")
        mean_ready = sem("mean_ready")
        var_eps_ready = sem("var_eps_ready")
        rstd_ready = sem("rstd_ready")
        normed_ready = sem("normed_ready")
        normedT_ready = sem("normedT_ready")
        hT_ready = sem("hT_ready")
        ctxT_turned = sem("ctxT_turned")
        ctxT_ready = sem("ctxT_ready")
        ctx_projected = sem("ctx_projected")
        ctx_projT_ready = sem("ctx_projT_ready")
        qk_projected = sem("qk_projected")
        rot_a_ready = sem("rot_a_ready")
        rot_b_ready = sem("rot_b_ready")
        qk_ready = sem("qk_ready")
        qk_rotated = sem("qk_rotated")
        v_projected = sem("v_projected")
        v_ready_act = sem("v_ready_act")
        v_ready_dve = sem("v_ready_dve")
        scores_ready = sem("scores_ready")
        top_ready = sem("top_ready")
        shifted_ready = sem("shifted_ready")
        turned_ready = sem("turned_ready")
        probs_ready = sem("probs_ready")
        o_ready = sem("o_ready")
        inv_ready = sem("inv_ready")
        o_normed = sem("o_normed")
        oT_turned = sem("oT_turned")
        oT_ready = sem("oT_ready")
        hidden_projected = sem("hidden_projected")
        gate_ready = sem("gate_ready")
        hidden_ready = sem("hidden_ready")
        glu_ready = sem("glu_ready")
        y_ready = sem("y_ready")
        x_biased_ready = sem("x_biased_ready")
        out_ready = sem("out_ready")
        stored = sem("stored")

        NORMS = SUBS + 1
        OT_OF = [G if HEAD[a // 2] == 64 else 1 for a in range(ATT)]
        OT_ALL = sum(OT_OF)
        PLAIN = G * sum(not ROPE[a // 2] for a in range(ATT))
        ROTATED = G * sum(ROPE[a // 2] for a in range(ATT))
        WIDE = sum(HEAD[a // 2] == 64 for a in range(ATT))

        def ot_before(a):
            return sum(OT_OF[:a])

        def plain_before(a):
            return G * sum(not ROPE[i // 2] for i in range(a))

        def rotated_before(a):
            return G * sum(ROPE[i // 2] for i in range(a))

        def wide_before(a):
            return sum(HEAD[i // 2] == 64 for i in range(a))

        def narrow(a):
            return HEAD[a // 2] == 8

        def sub_of(a):
            return 3 * (a // 2) + a % 2

        def wait_qk(eng, t, a, g):
            if ROPE[a // 2]:
                eng.wait_ge(qk_rotated, t * ROTATED + rotated_before(a) + g + 1)
            else:
                eng.wait_ge(qk_ready, t * PLAIN + plain_before(a) + g + 1)

        block = stack.enter_context(nc.Block())

        @block.sync
        def _(sp):
            sp.dma_start(sm[:], small).then_inc(small_loaded, 16)
            sp.dma_start(mod_w, mod_weights).then_inc(mod_w_loaded, 16)
            for s in range(SUBS):
                if s == MOD_HOME:
                    sp.wait_ge(mod_projected, 1)
                sp.dma_start(w_sb[s][:], weights[s]).then_inc(weights_loaded[s], 16)
            with sp.Fori(0, TURNS) as t:
                sp.wait_ge(inputs_taken, t)
                sp.wait_ge(ctx_taken, t)
                sp.dma_start(x_in[:], x[bass.ds(t * NB, NB)].rearrange("b n d -> n b d")).then_inc(inputs_loaded, 16)
                sp.dma_start(ctx_in[:], ctx[bass.ds(t * NB, NB)].rearrange("b n d -> n b d")).then_inc(inputs_loaded, 16)
            sp.wait_ge(stored, 16 * TURNS)

        @block.gpsimd
        def _(pool):
            nc.gpsimd.memset(minus_half[:], -0.5).then_inc(consts_ready, 1)
            nc.gpsimd.memset(epsilon[:, 0:NB], EPS[0]).then_inc(consts_ready, 1)
            nc.gpsimd.memset(epsilon[:, NB:2 * NB], EPS[LAYERS - 1]).then_inc(consts_ready, 1)
            nc.gpsimd.memset(v64[:], 1.0).then_inc(consts_ready, 1)
            nc.gpsimd.memset(v8[:], 1.0).then_inc(consts_ready, 1)
            pool.wait_ge(consts_ready, 5)
            pool.wait_ge(small_loaded, 16)

            def norm_scale(t, n, eps):
                eps_at = 0 if eps == EPS[0] else NB
                pool.wait_ge(mean_ready, t * NORMS + n + 1)
                nc.gpsimd.tensor_tensor(var_eps[:], mean_var[:, :, 1], epsilon[:, eps_at:eps_at + NB], ALU.add).then_inc(var_eps_ready, 1)
                pool.wait_ge(var_eps_ready, t * NORMS + n + 1)
                nc.gpsimd.tensor_tensor(rstd[:], var_eps[:], minus_half[:], ALU.pow).then_inc(rstd_ready, 1)

            with pool.Fori(0, TURNS) as t:
                norm_scale(t, 0, EPS[1])
                for s in range(SUBS):
                    layer, kind = divmod(s, 3)
                    norm_scale(t, 1 + s, EPS[layer])
                    bias = small_part("out_b")[:, s * P:(s + 1) * P]
                    nc.gpsimd.tensor_tensor(x_biased[:], xs[:], bias.unsqueeze(1).to_broadcast([P, NB, P]),
                                            ALU.add).then_inc(x_biased_ready, 1)
                    if kind < 2 and ROPE[layer]:
                        a = 2 * layer + kind
                        for g in range(G):
                            pool.wait_ge(rot_b_ready, t * ROTATED + rotated_before(a) + g + 1)
                            nc.gpsimd.tensor_tensor(qk[:, g % 2, :], rot_a[:], rot_b[:], ALU.add).then_inc(qk_rotated, 1)

        @block.scalar
        def _(act):
            act.wait_ge(small_loaded, 16)
            nc.scalar.activation(cond_silu[:], small_part("cond"), ACT.Silu).then_inc(silu_ready, 1)

            def modulate(t, s):
                act.wait_ge(normedT_ready, t * NORMS + s + 2)
                for b in range(NB):
                    last = nc.scalar.activation(hT[:, b * P:(b + 1) * P], ps[:, BACK, b * P:(b + 1) * P], ACT.Identity,
                                                bias=mod[:, b, s, 1:2], scale=mod[:, b, s, 0:1])
                last.then_inc(hT_ready, 1)

            def take_qk(t, a, g):
                act.wait_ge(qk_projected, t * ATT * G + a * G + g + 1)
                if QK_BIAS[a // 2][a % 2]:
                    for i in range(2):
                        at = (2 * a + i) * G + g
                        last = nc.scalar.activation(qk[:, g % 2, i * W:(i + 1) * W], ps[:, PROJ, i * W:(i + 1) * W],
                                                    ACT.Identity, bias=small_part("qk_b")[:, at:at + 1])
                else:
                    last = nc.scalar.copy(qk[:, g % 2, :], ps[:, PROJ, :])
                last.then_inc(qk_ready, 1)

            def take_v(t, a):
                act.wait_ge(v_projected, t * ATT + a + 1)
                src = ps[:, SCORE:SCORE + 2, :].rearrange("p c (h d) -> p (c h) d", d=64)
                nc.scalar.copy(v64[:, 0, :, 0:64], src).then_inc(v_ready_act, 1)

            def exps(t, a, g):
                n = t * ATT * G + a * G + g
                act.wait_ge(turned_ready, n + 1)
                nc.scalar.activation(probsT[:, g % 2, :, :], ps[:, TURNED, :].rearrange("p (j n) -> p j n", j=J),
                                     ACT.Exp, scale=float(HEAD[a // 2]) ** -0.5).then_inc(probs_ready, 1)

            def take_oT(t, a, g):
                act.wait_ge(oT_turned, t * OT_ALL + ot_before(a) + g + 1)
                nc.scalar.copy(oT[:, g, :, :], ps[:, BACK, 0:W].rearrange("p (b n) -> p b n", b=NB)).then_inc(oT_ready, 1)

            def attention(t, a):
                wide = not narrow(a)
                if not ROPE[a // 2]:
                    take_qk(t, a, 0)
                if wide:
                    take_v(t, a)
                for i in range(G + 3):
                    if i + 1 < G and not ROPE[a // 2]:
                        take_qk(t, a, i + 1)
                    if 0 <= i - 1 < G:
                        exps(t, a, i - 1)
                    if wide and 0 <= i - 3 < G:
                        take_oT(t, a, i - 3)
                if not wide:
                    take_oT(t, a, 0)

            def mlp(t, layer):
                for f in range(F):
                    n = t * LAYERS * F + layer * F + f
                    act.wait_ge(hidden_projected, n + 1)
                    at = (layer * 2 + GLU[layer]) * F + f
                    bias = small_part("h_b")[:, at:at + 1]
                    if GLU[layer]:
                        nc.scalar.activation(gate[:, f % 2, :], ps[:, SCORE + f % 2, W:2 * W], GELU[layer],
                                             bias=bias).then_inc(gate_ready, 1)
                    else:
                        nc.scalar.activation(hidden[:, f, :], ps[:, SCORE + f % 2, 0:W], GELU[layer],
                                             bias=bias).then_inc(hidden_ready, 1)

            act.wait_ge(silu_ready, 1)
            with act.Fori(0, TURNS) as t:
                act.wait_ge(ctxT_turned, t + 1)
                nc.scalar.copy(ctxT[:], ps[0:CD, PROJ, 0:W]).then_inc(ctxT_ready, 1)
                act.wait_ge(ctx_projected, t + 1)
                nc.scalar.activation(ctx_projT[:], ps[:, SCORE, 0:W], ACT.Identity,
                                     bias=small_part("ctx_b")).then_inc(ctx_projT_ready, 1)
                act.wait_ge(normedT_ready, t * NORMS + 1)
                nc.scalar.activation(ctx_normT[:], ps[0:CD, BACK, 0:W], ACT.Identity, bias=small_part("ctx_ln_b")[0:CD],
                                     scale=small_part("ctx_ln_w")[0:CD]).then_inc(hT_ready, 1)
                act.wait_ge(mod_ready, t + 2)
                for s in range(SUBS):
                    layer, kind = divmod(s, 3)
                    modulate(t, s)
                    if kind < 2:
                        attention(t, 2 * layer + kind)
                    else:
                        mlp(t, layer)
                act.wait_ge(out_ready, t + 1)
                act.dma_start(out[bass.ds(t * NB, NB)].rearrange("b n d -> n b d"), x_out[:]).then_inc(stored, 16)

        @block.vector
        def _(dve):
            dve.wait_ge(mod_projected, 1)
            dve.wait_ge(small_loaded, 16)
            proj = ps[:, PROJ, 0:2 * SUBS * B].rearrange("p (s k b) -> p s k b", s=SUBS, k=2)
            nc.vector.tensor_tensor(mod_sum[:].rearrange("p s k b -> p (s k) b"), proj.rearrange("p s k b -> p (s k) b"),
                                    small_part("mod_b").unsqueeze(2).to_broadcast([P, 2 * SUBS, B]),
                                    ALU.add).then_inc(mod_step, 1)
            dve.wait_ge(mod_step, 1)
            nc.vector.tensor_scalar(mod_gain[:], mod_sum[:, :, 0, :], 1.0, None, ALU.add).then_inc(mod_step, 1)
            dve.wait_ge(mod_step, 2)
            by_seq = mods[:].rearrange("p b s k -> p s k b")
            nc.vector.tensor_tensor(by_seq[:, :, 0, :], mod_gain[:],
                                    small_part("ln_w").unsqueeze(2).to_broadcast([P, SUBS, B]), ALU.mult).then_inc(mod_step, 1)
            nc.vector.tensor_tensor(mod_shift[:], mod_gain[:],
                                    small_part("ln_b").unsqueeze(2).to_broadcast([P, SUBS, B]), ALU.mult).then_inc(mod_step, 1)
            dve.wait_ge(mod_step, 4)
            nc.vector.tensor_tensor(by_seq[:, :, 1, :], mod_shift[:], mod_sum[:, :, 1, :], ALU.add).then_inc(mod_ready, 1)
            dve.wait_ge(mod_ready, 1)
            dve.wait_ge(consts_ready, 5)

            def norm(t, n, src, width):
                for b in range(NB):
                    last = nc.vector.bn_stats(stats[:, b, :], src[:, b, :])
                last.then_inc(stats_ready, 1)
                dve.wait_ge(stats_ready, t * NORMS + n + 1)
                nc.vector.tensor_copy(wait_taker[:], stats[:, 0, 0:1])
                for b in range(NB):
                    last = nc.vector.bn_aggr(mean_var[:, b, :], stats[:, b, :])
                last.then_inc(mean_ready, 1)
                dve.wait_ge(mean_ready, t * NORMS + n + 1)
                dve.wait_ge(rstd_ready, t * NORMS + n + 1)
                for b in range(NB):
                    last = nc.vector.tensor_scalar(normed[:, b, 0:width], src[:, b, :], mean_var[:, b, 0:1], rstd[:, b:b + 1],
                                                   ALU.subtract, ALU.mult)
                last.then_inc(normed_ready, 1)

            def rotate(t, a, g):
                n = t * ROTATED + rotated_before(a) + g
                dve.wait_ge(qk_projected, t * ATT * G + a * G + g + 1)
                dve.wait_ge(qk_rotated, n)
                for dst, bank, table, done in ((rot_a, PROJ, "cos", rot_a_ready), (rot_b, BACK, "sin", rot_b_ready)):
                    nc.vector.tensor_tensor(dst[:].rearrange("p (j n) -> p j n", n=P),
                                            ps[:, bank, :].rearrange("p (j n) -> p j n", n=P),
                                            small_part(table).unsqueeze(1).to_broadcast([P, 4, P]), ALU.mult).then_inc(done, 1)

            def take_v(t, a):
                dve.wait_ge(v_projected, t * ATT + a + 1)
                if narrow(a):
                    bias = small_part("v_b")[:, a * P:(a + 1) * P].rearrange("p (h d) -> p h d", h=H)
                    for b in range(NB):
                        last = nc.vector.tensor_tensor(v8[:, b, :, 0:8],
                                                       ps[:, SCORE + 2 * b, 0:P].rearrange("p (h d) -> p h d", h=H), bias, ALU.add)
                else:
                    src = ps[:, SCORE + 2:SCORE + 4, :].rearrange("p c (h d) -> p (c h) d", d=64)
                    last = nc.vector.tensor_copy(v64[:, 1, :, 0:64], src)
                last.then_inc(v_ready_dve, 1)

            def shift(t, a, g):
                n = t * ATT * G + a * G + g
                dve.wait_ge(scores_ready, n + 1)
                bank = SCORE + 2 * (g % 2)
                scores = ps[:, bank:bank + 2, 0:W].rearrange("p h (b m) -> p h b m", b=NB)
                tops = top[:, g % 2, :].rearrange("p (h b) -> p h b", h=2)
                nc.vector.tensor_reduce(tops, scores, AX.X, ALU.max).then_inc(top_ready, 1)
                dve.wait_ge(top_ready, n + 1)
                nc.vector.tensor_tensor(shifted[:, g % 2, :, :].rearrange("p (h b) m -> p h b m", h=2), scores,
                                        tops.unsqueeze(3).to_broadcast([P, 2, NB, P]),
                                        ALU.subtract).then_inc(shifted_ready, 1)

            def normalise(t, a, g):
                n = t * ATT * G + a * G + g
                d = HEAD[a // 2]
                dve.wait_ge(o_ready, n + 1)
                o = ps[:, OUT, 0:J * (d + 1)].rearrange("p (j d) -> p j d", j=J)
                nc.vector.reciprocal(inv[:, g % 2, :], o[:, :, d]).then_inc(inv_ready, 1)
                dve.wait_ge(inv_ready, n + 1)
                dst = o8[:, :, 16 * g:16 * g + 16] if narrow(a) else o64[:, g % 2, :, :]
                nc.vector.tensor_tensor(dst.rearrange("p b (h d) -> p h b d", h=2),
                                        o[:, :, 0:d].rearrange("p (h b) d -> p h b d", h=2),
                                        inv[:, g % 2, :].rearrange("p (h b) -> p h b", h=2).unsqueeze(3)
                                        .to_broadcast([P, 2, NB, d]), ALU.mult).then_inc(o_normed, 1)

            def attention(t, a):
                if ROPE[a // 2]:
                    rotate(t, a, 0)
                take_v(t, a)
                for i in range(G + 2):
                    if i + 1 < G and ROPE[a // 2]:
                        rotate(t, a, i + 1)
                    if i < G:
                        shift(t, a, i)
                    if 0 <= i - 2 < G:
                        normalise(t, a, i - 2)

            def glu(t, layer):
                for f in range(F):
                    dve.wait_ge(gate_ready, t * F + f + 1)
                    at = layer * 2 * F + f
                    nc.vector.scalar_tensor_tensor(out=hidden[:, f, :], in0=ps[:, SCORE + f % 2, 0:W],
                                                   scalar=small_part("h_b")[:, at:at + 1], in1=gate[:, f % 2, :],
                                                   op0=ALU.add, op1=ALU.mult).then_inc(glu_ready, 1)

            with dve.Fori(0, TURNS) as t:
                dve.wait_ge(inputs_loaded, t * 32 + 32)
                nc.vector.tensor_copy(mod[:].rearrange("p b s k -> p (b s k)"),
                                      mods[:].rearrange("p b s k -> p (b s k)")[:, bass.ds(t * (NB * SUBS * 2), NB * SUBS * 2)]
                                      ).then_inc(mod_ready, 1)
                nc.vector.tensor_copy(xs[:], x_in[:]).then_inc(x_ready, 1)
                norm(t, 0, ctx_in, CD)
                dve.wait_ge(normed_ready, t * NORMS + 1)
                dve.wait_ge(normedT_ready, t * NORMS + 1)
                dve.wait_ge(x_ready, t * SUBS + 1)
                for s in range(SUBS):
                    layer, kind = divmod(s, 3)
                    norm(t, 1 + s, xs, P)
                    if s == 0:
                        nc.vector.tensor_copy(stats[:, 0, 0:1], mean_var[:, 0, 0:1]).then_inc(inputs_taken, 1)
                    if kind < 2:
                        attention(t, 2 * layer + kind)
                    elif GLU[layer]:
                        glu(t, layer)
                    dve.wait_ge(y_ready, t * SUBS + s + 1)
                    dve.wait_ge(x_biased_ready, t * SUBS + s + 1)
                    last_sub = s == SUBS - 1
                    if last_sub:
                        dve.wait_ge(stored, t * 16)
                    nc.vector.tensor_tensor(x_out[:] if last_sub else xs[:], ps[:, TURNED:TURNED + 2, 0:P], x_biased[:],
                                            ALU.add).then_inc(out_ready if last_sub else x_ready, 1)
                    if not last_sub:
                        dve.wait_ge(x_ready, t * SUBS + s + 2)
                    else:
                        dve.wait_ge(out_ready, t + 1)

        @block.tensor
        def _(pe):
            mm = nc.tensor.matmul
            pe.wait_ge(small_loaded, 16)
            pe.wait_ge(mod_w_loaded, 16)
            pe.wait_ge(silu_ready, 1)
            for s in range(SUBS):
                for k in range(2):
                    at = 2 * s + k
                    src = cond_silu[:] if s // 3 in (0, 3) else small_part("cond")
                    last = mm(ps[:, PROJ, at * B:(at + 1) * B], mod_w[:, at * P:(at + 1) * P], src,
                              start=True, stop=True)
            last.then_inc(mod_projected, 1)

            def turn_norm(t, n, width):
                pe.wait_ge(normed_ready, t * NORMS + n + 1)
                for b in range(NB):
                    last = nc.tensor.transpose(ps[0:width, BACK, b * P:(b + 1) * P], normed[:, b, 0:width], ident)
                last.then_inc(normedT_ready, 1)

            def kv_source(a):
                if a % 2 == 0:
                    return hT, P
                return [(ctxT, CD), (ctx_normT, CD), (ctxT, CD), (ctx_projT, P)][a // 2]

            def project_qk(t, a, g):
                s, (kv, depth) = sub_of(a), kv_source(a)
                n = t * ATT * G + a * G + g
                if ROPE[a // 2]:
                    if g:
                        pe.wait_ge(rot_b_ready, t * ROTATED + rotated_before(a) + g)
                    if g >= 5:
                        pe.wait_ge(oT_ready, t * OT_ALL + ot_before(a) + g - 4)
                    passes = (("q", "k", PROJ), ("q_swapped", "k_swapped", BACK))
                else:
                    if g:
                        pe.wait_ge(qk_ready, t * PLAIN + plain_before(a) + g)
                    passes = (("q", "k", PROJ),)
                cols = slice(g * P, (g + 1) * P)
                for q_name, k_name, bank in passes:
                    mm(ps[:, bank, 0:W], weight(s, q_name)[:, cols], hT[:], start=True, stop=True)
                    last = mm(ps[:, bank, W:2 * W], weight(s, k_name)[0:depth, cols], kv[0:depth, :], start=True, stop=True)
                last.then_inc(qk_projected, 1)

            def project_v(t, a):
                s, (kv, depth) = sub_of(a), kv_source(a)
                for b in range(NB):
                    if narrow(a):
                        last = mm(ps[:, SCORE + 2 * b, 0:P], kv[0:depth, b * P:(b + 1) * P], weight(s, "v")[0:depth, :],
                                  start=True, stop=True)
                    else:
                        for c in range(2):
                            last = mm(ps[:, SCORE + 2 * b + c, :], kv[0:depth, b * P:(b + 1) * P],
                                      weight(s, "v")[0:depth, c * 512:(c + 1) * 512], start=True, stop=True)
                last.then_inc(v_projected, 1)

            def scores(t, a, g):
                n = t * ATT * G + a * G + g
                wait_qk(pe, t, a, g)
                if g == 0:
                    pe.wait_ge(v_ready_dve, t * ATT + a + 1)
                    if not narrow(a):
                        pe.wait_ge(v_ready_act, t * WIDE + wide_before(a) + 1)
                if g >= 2:
                    pe.wait_ge(shifted_ready, n - 1)
                for h in range(2):
                    rows = slice(HALF * h, HALF * h + HALF)
                    for b in range(NB):
                        last = mm(ps[:, SCORE + 2 * (g % 2) + h, b * P:(b + 1) * P], qk[rows, g % 2, b * P:(b + 1) * P],
                                  qk[rows, g % 2, W + b * P:W + (b + 1) * P], start=True, stop=True)
                last.then_inc(scores_ready, 1)

            def turn_shifted(t, a, g):
                n = t * ATT * G + a * G + g
                pe.wait_ge(shifted_ready, n + 1)
                if g:
                    pe.wait_ge(probs_ready, n)
                for j in range(J):
                    last = nc.tensor.transpose(ps[:, TURNED, j * P:(j + 1) * P], shifted[:, g % 2, j, :], ident)
                last.then_inc(turned_ready, 1)

            def apply_probs(t, a, g):
                n = t * ATT * G + a * G + g
                d = HEAD[a // 2]
                v = v8 if narrow(a) else v64
                pe.wait_ge(probs_ready, n + 1)
                if g:
                    pe.wait_ge(o_normed, n)
                for h in range(2):
                    for b in range(NB):
                        j = NB * h + b
                        last = mm(ps[:, OUT, j * (d + 1):(j + 1) * (d + 1)], probsT[:, g % 2, j, :],
                                  v[:, b, 2 * g + h, :], start=True, stop=True)
                last.then_inc(o_ready, 1)

            def turn_back(t, a, g):
                pe.wait_ge(o_normed, t * ATT * G + a * G + (G if narrow(a) else g + 1))
                if ROPE[a // 2] and g + 4 < G:
                    pe.wait_ge(rot_b_ready, t * ROTATED + rotated_before(a) + g + 5)
                elif g:
                    pe.wait_ge(oT_ready, t * OT_ALL + ot_before(a) + g)
                for b in range(NB):
                    src = o8[:, b, :] if narrow(a) else o64[:, g % 2, b, :]
                    last = nc.tensor.transpose(ps[:, BACK, b * P:(b + 1) * P], src, ident)
                last.then_inc(oT_turned, 1)

            def attention(t, a):
                s = sub_of(a)
                project_qk(t, a, 0)
                project_v(t, a)
                for i in range(G + 3):
                    if i + 1 < G:
                        project_qk(t, a, i + 1)
                    if i < G:
                        scores(t, a, i)
                    if 0 <= i - 1 < G:
                        turn_shifted(t, a, i - 1)
                    if not narrow(a) and 0 <= i - 3 < G:
                        turn_back(t, a, i - 3)
                    if 0 <= i - 2 < G:
                        apply_probs(t, a, i - 2)
                if narrow(a):
                    turn_back(t, a, 0)
                blocks = OT_OF[a]
                pe.wait_ge(oT_ready, t * OT_ALL + ot_before(a) + blocks)
                for b in range(NB):
                    for c in range(blocks):
                        last = mm(ps[:, TURNED + b, 0:P], oT[:, c, b, :], weight(s, "o")[:, c * P:(c + 1) * P],
                                  start=(c == 0), stop=(c == blocks - 1))
                last.then_inc(y_ready, 1)

            def wait_hidden(t, layer, f):
                if GLU[layer]:
                    pe.wait_ge(glu_ready, t * F + f + 1)
                else:
                    done = F * sum(not GLU[i] for i in range(layer))
                    pe.wait_ge(hidden_ready, t * F * sum(not g for g in GLU) + done + f + 1)

            def mlp(t, layer):
                s = 3 * layer + 2

                def up(f):
                    for i in range(2 if GLU[layer] else 1):
                        last = mm(ps[:, SCORE + f % 2, i * W:(i + 1) * W],
                                  weight(s, "w1")[:, (i * F + f) * P:(i * F + f + 1) * P], hT[:], start=True, stop=True)
                    last.then_inc(hidden_projected, 1)

                up(0)
                up(1)
                for f in range(F):
                    wait_hidden(t, layer, f)
                    if f + 2 < F:
                        up(f + 2)
                    for b in range(NB):
                        last = mm(ps[:, TURNED + b, 0:P], hidden[:, f, b * P:(b + 1) * P], weight(s, "w2")[:, f * P:(f + 1) * P],
                                  start=(f == 0), stop=(f == F - 1))
                last.then_inc(y_ready, 1)

            pe.wait_ge(mod_ready, 1)
            with pe.Fori(0, TURNS) as t:
                pe.wait_ge(inputs_loaded, t * 32 + 32)
                for b in range(NB):
                    last = nc.tensor.transpose(ps[0:CD, PROJ, b * P:(b + 1) * P], ctx_in[:, b, :], ident)
                last.then_inc(ctxT_turned, 1)
                pe.wait_ge(ctxT_ready, t + 1)
                mm(ps[:, SCORE, 0:W], small_part("ctx_w")[0:CD, :], ctxT[:], start=True, stop=True).then_inc(ctx_projected, 1)
                turn_norm(t, 0, CD)
                pe.wait_ge(ctx_projT_ready, t + 1)
                for s in range(SUBS):
                    layer, kind = divmod(s, 3)
                    pe.wait_ge(hT_ready, t * NORMS + s + 1)
                    turn_norm(t, 1 + s, P)
                    pe.wait_ge(weights_loaded[s], 16)
                    pe.wait_ge(hT_ready, t * NORMS + s + 2)
                    if s == 0:
                        nc.tensor.transpose(ps[0:CD, BACK, 0:P], ctx_in[:, 0, :], ident).then_inc(ctx_taken, 1)
                    if kind < 2:
                        attention(t, 2 * layer + kind)
                    else:
                        mlp(t, layer)


def pack_weights(inputs):
    import numpy as np

    def rows(a):
        a = np.asarray(a)
        full = np.zeros((P, a.shape[1]), a.dtype)
        full[:a.shape[0]] = a
        return full

    def spread(a):
        a = rows(a).reshape(P, G, 2, 8)
        full = np.zeros((P, G, 2, HALF), a.dtype)
        full[..., :8] = a
        return full.reshape(P, G * P)

    def swapped(a):
        return rows(a).reshape(P, -1, 2)[:, :, ::-1].reshape(P, -1)

    def blocks(a):
        a = np.asarray(a)
        return a.reshape(-1, P, a.shape[1]).transpose(1, 0, 2).reshape(P, -1)

    L0, L1, L2, L3 = ({k[9:]: v for k, v in inputs.items() if k.startswith(f"L{i}_xcond_")} for i in range(4))
    q0, k0, v0 = np.split(np.asarray(L0["Wqkv"]), 3, axis=1)
    q3, k3, v3 = np.split(np.asarray(L3["W_qkv"]), 3, axis=1)
    sk, sv = np.split(np.asarray(L1["sa_wkv"]), 2, axis=1)
    ck, cv = np.split(np.asarray(L1["ca_wkv"]), 2, axis=1)
    parts = [
        [spread(q0), spread(k0), rows(v0), blocks(L0["Wos"])],
        [spread(L0["Wq"]), spread(L0["Wk"]), rows(L0["Wv"]), blocks(L0["Woc"])],
        [rows(L0["W1"]), blocks(L0["W2"])],
        [rows(L1["sa_wq"]), rows(sk), rows(sv), blocks(L1["sa_wo"]), swapped(L1["sa_wq"]), swapped(sk)],
        [rows(L1["ca_wq"]), rows(ck), rows(cv), blocks(L1["ca_wo"]), swapped(L1["ca_wq"]), swapped(ck)],
        [rows(L1["ff_w1"]), blocks(L1["ff_w2"])],
        [rows(L2["q1"]), rows(L2["k1"]), rows(L2["v1"]), blocks(L2["o1_w"])],
        [rows(L2["q2"]), rows(L2["k2"]), rows(L2["v2"]), blocks(L2["o2_w"])],
        [rows(L2["ff_w1"]), blocks(L2["ff_w2"])],
        [spread(q3), spread(k3), rows(v3), blocks(L3["W_proj"])],
        [spread(L3["W_q"]), spread(L3["W_k"]), rows(L3["W_v"]), blocks(L3["W_out"])],
        [rows(L3["W_fc1"]), blocks(L3["W_fc2"])],
    ]
    return [np.ascontiguousarray(np.concatenate(p, axis=1)) for p in parts]


def pack_small(inputs):
    import numpy as np

    L0, L1, L2, L3 = ({k[9:]: np.asarray(v) for k, v in inputs.items() if k.startswith(f"L{i}_xcond_")} for i in range(4))
    where, width = small_columns()
    full = np.zeros((P, width), np.float32)
    mod_w = np.zeros((P, 2 * SUBS * P), np.float32)

    def put(name, a, at=0):
        a = np.asarray(a)
        start = where[name][0] + at
        full[:a.shape[0], start:start + a.shape[1]] = a

    def cols(a):
        return np.asarray(a).reshape(-1, P).T

    def everywhere(a):
        return np.broadcast_to(np.asarray(a).reshape(1, -1), (P, np.asarray(a).size))

    put("ident", np.eye(P, dtype=np.float32))
    put("cond", np.asarray(inputs["cond_1024"]).T)
    m0, c0 = L0["Wmod"], L0["bmod"]
    m3, c3 = L3["W_ada"], L3["b_ada"]
    part = lambda a, i: a[..., i * P:(i + 1) * P]
    pairs = [(m0, c0, 1), (m0, c0, 0), (m0, c0, 3), (m0, c0, 2), (m0, c0, 5), (m0, c0, 4)]
    pairs += [(L1["g1_w"], L1["g1_b"], 0), (L1["b1_w"], L1["b1_b"], 0)] * 2
    pairs += [(L1["g2_w"], L1["g2_b"], 0), (L1["b2_w"], L1["b2_b"], 0)]
    for n in "123":
        pairs += [(L2[f"n{n}_w"], L2[f"n{n}_b"], 0), (L2[f"n{n}_w"], L2[f"n{n}_b"], 1)]
    pairs += [(m3, c3, 1), (m3, c3, 0), (m3, c3, 3), (m3, c3, 2), (m3, c3, 5), (m3, c3, 4)]
    for n, (w, b, i) in enumerate(pairs):
        mod_w[:, n * P:(n + 1) * P] = part(w, i)
        put("mod_b", cols(part(b, i)), n)
    norms = [("ln1", L0), ("ln2", L0), ("ln3", L0), ("ln1", L1), ("ln1", L1), ("ln2", L1)]
    for s in range(SUBS):
        if s < len(norms):
            name, layer = norms[s]
            put("ln_w", cols(layer[name + "_w"]), s)
            put("ln_b", cols(layer[name + "_b"]), s)
        else:
            put("ln_w", np.ones((P, 1), np.float32), s)
    put("ctx_w", L3["W_ctx"])
    put("ctx_b", cols(L3["b_ctx"]))
    put("ctx_ln_w", L1["ca_lnc_w"].reshape(CD, 1))
    put("ctx_ln_b", L1["ca_lnc_b"].reshape(CD, 1))
    d = 64
    inv_freq = np.float32(1.0) / np.float32(10000.0) ** (np.arange(0, d, 2, dtype=np.float32) / np.float32(d))
    angle = np.arange(P, dtype=np.float32)[None, :] * inv_freq[:, None]
    put("cos", np.tile(np.repeat(np.cos(angle), 2, axis=0), (2, 1)))
    put("sin", np.tile(np.stack([-np.sin(angle), np.sin(angle)], axis=1).reshape(d, P), (2, 1)))

    def halves(a):
        out = np.zeros((2, HALF, G), np.float32)
        out[:, :8] = np.asarray(a).reshape(G, 2, 8).transpose(1, 2, 0)
        return out.reshape(P, G)

    bq0, bk0, bv0 = np.split(L0["bqkv"], 3)
    bq3, bk3, bv3 = np.split(L3["b_qkv"], 3)
    for a, (bq, bk, bv) in {0: (bq0, bk0, bv0), 1: (L0["bq"], L0["bk"], L0["bv"]), 6: (bq3, bk3, bv3)}.items():
        put("qk_b", halves(bq), 2 * a * G)
        put("qk_b", halves(bk), (2 * a + 1) * G)
        put("v_b", everywhere(bv), a * P)
    outs = [L0["bos"], L0["boc"], L0["b2"], L1["sa_bo"], L1["ca_bo"], L1["ff_b2"],
            L2["o1_b"], L2["o2_b"], L2["ff_b2"], L3["b_proj"], L3["b_out"], L3["b_fc2"]]
    for s, b in enumerate(outs):
        put("out_b", everywhere(b), s * P)
    for layer, b in enumerate([L0["b1"], L1["ff_b1"], L2["ff_b1"], L3["b_fc1"]]):
        put("h_b", cols(b), layer * 2 * F)
    return full, mod_w


def kernel(**inputs):
    import numpy as np
    from concourse import bacc
    from concourse.bass_utils import run_bass_kernel_spmd

    arrays = {
        "x_dram": np.ascontiguousarray(inputs["x"]),
        "ctx_dram": np.ascontiguousarray(inputs["ctx_768"]),
    }
    arrays["small_dram"], arrays["mod_w_dram"] = pack_small(inputs)
    for s, w in enumerate(pack_weights(inputs)):
        arrays[f"weights{s}_dram"] = w
    nc = bacc.Bacc("TRN2", target_bir_lowering=False, num_devices=1)
    aps = {n: nc.dram_tensor(n, a.shape, mybir.dt.from_np(a.dtype), kind="ExternalInput").ap() for n, a in arrays.items()}
    out = nc.dram_tensor("out_dram", (B, P, P), F32, kind="ExternalOutput").ap()
    build(nc, aps["x_dram"], aps["ctx_dram"], aps["small_dram"], aps["mod_w_dram"],
          [aps[f"weights{s}_dram"] for s in range(SUBS)], out)
    r = run_bass_kernel_spmd(nc, [arrays], core_ids=[0])
    return r.results[0]["out_dram"]
```

```python
from contextlib import ExitStack

import concourse.bass as bass
from concourse import mybir

ALU = mybir.AluOpType
ACT = mybir.ActivationFunctionType
AX = mybir.AxisListType
F32 = mybir.dt.float32

P = 128
B = 8
NB = 2
STREAMS = 2
TURNS = B // (NB * STREAMS)
W = NB * P
CD = 96
H = 16
G = 8
J = 2 * NB
LAYERS = 4
SUBS = 3 * LAYERS
ATT = 2 * LAYERS
F = 4
HALF = 64

HEAD = [8, 64, 64, 8]
ROPE = [False, True, False, False]
GLU = [False, False, True, False]
EPS = [1e-5, 1e-5, 1e-5, 1e-6]
GELU = [ACT.Gelu, ACT.Gelu, ACT.Gelu, ACT.Gelu_apprx_tanh]
PAIR_SWAP = [i ^ 1 for i in range(32)]

CONTEXT_STEPS = 2
NORM_STEPS = 2
LAGS = 3
ATTENTION_STEPS = 1 + G + LAGS + 1
MLP_STEPS = 3
STEPS = CONTEXT_STEPS + LAYERS * (3 * NORM_STEPS + 2 * ATTENTION_STEPS + MLP_STEPS) + 1
BEHIND = 8


def interleave(first, second):
    for n in range(STEPS + BEHIND):
        if n < STEPS:
            next(first)
        if n >= BEHIND:
            next(second)
    assert next(first, None) is None and next(second, None) is None


def narrow(a):
    return HEAD[a // 2] == 8


def sub_of(a):
    return 3 * (a // 2) + a % 2


def weight_columns(s):
    layer, kind = divmod(s, 3)
    if kind == 2:
        parts = [("w1", F * P * (2 if GLU[layer] else 1)), ("w2", F * P)]
    else:
        width = H * HEAD[layer]
        parts = [("q", width), ("k", width), ("v", width), ("o", width)]
    at, where = 0, {}
    for name, width in parts:
        where[name] = (at, width)
        at += width
    return where, at


def small_columns():
    parts = [("ident", P), ("cond", B), ("mod_b", 2 * SUBS), ("ln_w", SUBS), ("ln_b", SUBS),
             ("ctx_w", P), ("ctx_b", 1), ("ctx_ln_w", 1), ("ctx_ln_b", 1), ("cos", P), ("sin", P), ("head_mask", H), ("half_mask", 2),
             ("qk_b", 2 * ATT), ("v_b", 4 * P), ("out_b", SUBS * P), ("h_b", LAYERS * 2 * F)]
    at, where = 0, {}
    for name, width in parts:
        where[name] = (at, width)
        at += width
    return where, at


def build(nc, x, ctx, small, mod_weights, weights, out):
    s_at, s_width = small_columns()
    w_at = [weight_columns(s) for s in range(SUBS)]

    with ExitStack() as stack:
        def sb(name, shape):
            return stack.enter_context(nc.sbuf_tensor(name, shape, F32))

        def sem(name):
            return stack.enter_context(nc.semaphore(name))

        def sb2(name, shape):
            return [sb(f"{name}_{c}", shape) for c in range(STREAMS)]

        def sem2(name):
            return [sem(f"{name}_{c}") for c in range(STREAMS)]

        sm = sb("small_sb", [P, s_width])
        w_sb = [sb(f"w_sb{s}", [P, w_at[s][1]]) for s in range(SUBS)]

        def small_part(name):
            a, n = s_at[name]
            return sm[:, a:a + n]

        def weight(s, name):
            a, n = w_at[s][0][name]
            return w_sb[s][:, a:a + n]

        ident = small_part("ident")
        MOD_HOME = 3
        mod_w = w_sb[MOD_HOME][:, 0:2 * SUBS * P]
        cond_silu = sb("cond_silu", [P, B])
        mod_sum = sb("mod_sum", [P, SUBS, 2, B])
        mod_gain = sb("mod_gain", [P, SUBS, B])
        mod_shift = sb("mod_shift", [P, SUBS, B])
        mods = sb("mods", [P, B, SUBS, 2])
        minus_half = sb("minus_half", [P, NB])
        epsilon = sb("epsilon", [P, 2 * NB])
        wait_taker = sb("wait_taker", [P, 1])
        mod = sb2("mod", [P, NB, SUBS, 2])
        x_in = sb2("x_in", [P, NB, P])
        ctx_in = sb2("ctx_in", [P, NB, CD])
        xs = sb2("xs", [P, NB, P])
        x_biased = sb2("x_biased", [P, NB, P])
        x_out = sb2("x_out", [P, NB, P])
        stats = sb2("stats", [P, NB, 6])
        mean_var = sb2("mean_var", [P, NB, 2])
        var_eps = sb2("var_eps", [P, NB])
        rstd = sb2("rstd", [P, NB])
        normed = sb2("normed", [P, NB, P])
        hT = sb2("hT", [P, W])
        ctxT = sb2("ctxT", [CD, W])
        ctx_normT = sb2("ctx_normT", [CD, W])
        ctx_projT = sb2("ctx_projT", [P, W])
        qk = sb2("qk", [P, 2, 2 * W])
        k_head = sb2("k_head", [P, 2, 2, W])
        rot_a = sb2("rot_a", [P, 2 * W])
        rot_swap = sb2("rot_swap", [P, 2 * W])
        rot_b = sb2("rot_b", [P, 2 * W])
        v64 = sb2("v64", [P, NB, H, 65])
        v8 = sb2("v8", [P, NB, H, 9])
        top = sb2("top", [P, 2, J])
        shifted = sb2("shifted", [P, 2, J, P])
        probsT = sb2("probsT", [P, 2, J, P])
        inv = sb2("inv", [P, 2, J])
        o64 = sb2("o64", [P, 2, NB, P])
        o8 = sb2("o8", [P, NB, P])
        oT = sb2("oT", [P, G, NB, P])
        hidden = [o[:].rearrange("p g b n -> p g (b n)")[:, 0:F, :] for o in oT]
        gate = [o[:].rearrange("p g b n -> p g (b n)")[:, F:2 * F, :] for o in oT]

        ps = stack.enter_context(nc.psum_tensor("ps", [P, 8, 512], F32))
        BANKS = 4
        PROJ, SCORE, TURNED, OUT = range(BANKS)

        def bank(c, n, count=None):
            return ps[:, BANKS * c + n, :] if count is None else ps[:, BANKS * c + n:BANKS * c + n + count, :]

        small_loaded = sem("small_loaded")
        mod_w_loaded = sem("mod_w_loaded")
        weights_loaded = [sem(f"weights_loaded{s}") for s in range(SUBS)]
        consts_ready = sem("consts_ready")
        silu_ready = sem("silu_ready")
        mod_projected = sem("mod_projected")
        mod_step = sem("mod_step")
        mods_ready = sem("mods_ready")
        inputs_loaded = sem2("inputs_loaded")
        inputs_taken = sem2("inputs_taken")
        ctx_taken = sem2("ctx_taken")
        mod_ready = sem2("mod_ready")
        x_ready = sem2("x_ready")
        stats_ready = sem2("stats_ready")
        mean_ready = sem2("mean_ready")
        var_eps_ready = sem2("var_eps_ready")
        rstd_ready = sem2("rstd_ready")
        normed_ready = sem2("normed_ready")
        normedT_ready = sem2("normedT_ready")
        hT_ready = sem2("hT_ready")
        ctxT_ready = sem2("ctxT_ready")
        ctx_projected = sem2("ctx_projected")
        ctx_projT_ready = sem2("ctx_projT_ready")
        qk_projected = sem2("qk_projected")
        qk_taken = sem2("qk_taken")
        rot_a_ready = sem2("rot_a_ready")
        rot_b_ready = sem2("rot_b_ready")
        k_cleared = sem2("k_cleared")
        k_masked = sem2("k_masked")
        qk_rotated = sem2("qk_rotated")
        v_projected = sem2("v_projected")
        v_taken_act = sem2("v_taken_act")
        v_taken_dve = sem2("v_taken_dve")
        scores_ready = sem2("scores_ready")
        top_ready = sem2("top_ready")
        shifted_ready = sem2("shifted_ready")
        turned_ready = sem2("turned_ready")
        probs_ready = sem2("probs_ready")
        o_ready = sem2("o_ready")
        inv_ready = sem2("inv_ready")
        o_normed = sem2("o_normed")
        oT_turned = sem2("oT_turned")
        oT_ready = sem2("oT_ready")
        hidden_projected = sem2("hidden_projected")
        gate_ready = sem2("gate_ready")
        hidden_ready = sem2("hidden_ready")
        glu_ready = sem2("glu_ready")
        y_ready = sem2("y_ready")
        x_biased_ready = sem2("x_biased_ready")
        out_ready = sem2("out_ready")
        stored = sem2("stored")

        NORMS = SUBS + 1
        NG = ATT * G

        def before(a, kind, each):
            return each * sum(kind(i) for i in range(a))

        def rotary(a):
            return ROPE[a // 2]

        def masked(a):
            return narrow(a) or rotary(a)

        def wide(a):
            return not narrow(a)

        def qk_count(a):
            return 1 if narrow(a) else G

        def ot_count(a):
            return 1 if narrow(a) else G

        def v_parts(a):
            return 1 if narrow(a) else 2

        def group(t, a, g):
            return t * NG + a * G + g

        def at_rotated(t, a, g):
            return t * before(ATT, rotary, G) + before(a, rotary, G) + g

        def at_masked(t, a, g):
            return t * before(ATT, masked, G) + before(a, masked, G) + g

        def at_qk(t, a, g):
            return t * before(ATT, qk_count, 1) + before(a, qk_count, 1) + g

        def at_ot(t, a, g):
            return t * before(ATT, ot_count, 1) + before(a, ot_count, 1) + g

        def at_v(t, a, n):
            return t * before(ATT, v_parts, 1) + before(a, v_parts, 1) + n

        def at_wide(t, a):
            return t * before(ATT, wide, 1) + before(a, wide, 1)

        def first_sequence(t, c):
            return (t * STREAMS + c) * NB

        block = stack.enter_context(nc.Block())

        @block.sync
        def _(sp):
            sp.dma_start(sm[:], small).then_inc(small_loaded, 16)
            sp.dma_start(mod_w, mod_weights).then_inc(mod_w_loaded, 16)
            with sp.Fori(0, TURNS) as t:
                for c in range(STREAMS):
                    sp.wait_ge(inputs_taken[c], t)
                    sp.wait_ge(ctx_taken[c], t)
                    for dst, src in ((x_in[c], x), (ctx_in[c], ctx)):
                        sp.dma_start(dst[:], src[bass.ds(first_sequence(t, c), NB)].rearrange("b n d -> n b d")
                                     ).then_inc(inputs_loaded[c], 16)
            for c in range(STREAMS):
                sp.wait_ge(stored[c], 16 * TURNS)

        @block.gpsimd
        def _(pool):
            nc.gpsimd.memset(minus_half[:], -0.5).then_inc(consts_ready, 1)
            nc.gpsimd.memset(epsilon[:, 0:NB], EPS[0]).then_inc(consts_ready, 1)
            nc.gpsimd.memset(epsilon[:, NB:2 * NB], EPS[LAYERS - 1]).then_inc(consts_ready, 1)
            for c in range(STREAMS):
                nc.gpsimd.memset(v64[c][:], 1.0).then_inc(consts_ready, 1)
                nc.gpsimd.memset(v8[c][:], 1.0).then_inc(consts_ready, 1)
            pool.wait_ge(consts_ready, 3 + 2 * STREAMS)
            pool.wait_ge(small_loaded, 16)

            def norm_scale(t, c, n, layer):
                at = NB if EPS[layer] != EPS[0] else 0
                pool.wait_ge(mean_ready[c], t * NORMS + n + 1)
                nc.gpsimd.tensor_tensor(var_eps[c][:], mean_var[c][:, :, 1], epsilon[:, at:at + NB],
                                        ALU.add).then_inc(var_eps_ready[c], 1)
                pool.wait_ge(var_eps_ready[c], t * NORMS + n + 1)
                nc.gpsimd.tensor_tensor(rstd[c][:], var_eps[c][:], minus_half[:], ALU.pow).then_inc(rstd_ready[c], 1)

            def add_bias(t, c, s):
                bias = small_part("out_b")[:, s * P:(s + 1) * P]
                nc.gpsimd.tensor_tensor(x_biased[c][:], xs[c][:], bias.unsqueeze(1).to_broadcast([P, NB, P]),
                                        ALU.add).then_inc(x_biased_ready[c], 1)

            def clear_k(t, c):
                pool.wait_ge(scores_ready[c], group(t, 4, 0))
                some = ident.unsqueeze(1).to_broadcast([P, 2 * 2 * NB, P])
                nc.gpsimd.tensor_tensor(k_head[c][:].rearrange("p i h (b n) -> p (i h b) n", b=NB), some, some,
                                        ALU.subtract).then_inc(k_cleared[c], 1)

            def mask_k(t, c, a, g):
                if g >= 2:
                    pool.wait_ge(scores_ready[c], group(t, a, g - 1))
                if narrow(a):
                    pool.wait_ge(qk_taken[c], at_qk(t, a, 1))
                    mask, k = small_part("head_mask")[:, 2 * g:2 * g + 2], qk[c][:, 0, W:2 * W]
                else:
                    pool.wait_ge(qk_rotated[c], at_rotated(t, a, g) + 1)
                    mask, k = small_part("half_mask"), qk[c][:, g % 2, W:2 * W]
                nc.gpsimd.tensor_tensor(k_head[c][:, g % 2, :, :], k.unsqueeze(1).to_broadcast([P, 2, W]),
                                        mask.unsqueeze(2).to_broadcast([P, 2, W]), ALU.mult).then_inc(k_masked[c], 1)

            def rotate(t, c, a, g):
                pool.wait_ge(rot_b_ready[c], at_rotated(t, a, g) + 1)
                nc.gpsimd.tensor_tensor(qk[c][:, g % 2, :], rot_a[c][:], rot_b[c][:], ALU.add).then_inc(qk_rotated[c], 1)
                mask_k(t, c, a, g)

            def stream(t, c):
                norm_scale(t, c, 0, 1)
                yield
                yield
                for s in range(SUBS):
                    layer, kind = divmod(s, 3)
                    a = 2 * layer + kind
                    norm_scale(t, c, 1 + s, layer)
                    add_bias(t, c, s)
                    yield
                    if s == 6:
                        clear_k(t, c)
                    yield
                    if kind == 2:
                        for _ in range(MLP_STEPS):
                            yield
                        continue
                    make_k = mask_k if narrow(a) else rotate if rotary(a) else None
                    for g in range(G + LAGS + 2):
                        if make_k and g < G:
                            make_k(t, c, a, g)
                        yield
                yield

            with pool.Fori(0, TURNS) as t:
                interleave(stream(t, 0), stream(t, 1))

        @block.scalar
        def _(act):
            act.wait_ge(small_loaded, 16)
            nc.scalar.activation(cond_silu[:], small_part("cond"), ACT.Silu).then_inc(silu_ready, 1)
            for s in range(SUBS):
                if s == MOD_HOME:
                    act.wait_ge(mod_projected, 1)
                act.dma_start(w_sb[s][:], weights[s]).then_inc(weights_loaded[s], 16)
            act.wait_ge(silu_ready, 1)

            def modulate(t, c, s):
                act.wait_ge(mod_ready[c], t + 1)
                act.wait_ge(normedT_ready[c], t * NORMS + s + 2)
                for b in range(NB):
                    last = nc.scalar.activation(hT[c][:, b * P:(b + 1) * P], bank(c, PROJ)[:, b * P:(b + 1) * P], ACT.Identity,
                                                bias=mod[c][:, b, s, 1:2], scale=mod[c][:, b, s, 0:1])
                last.then_inc(hT_ready[c], 1)

            def take_qk(t, c, a, g):
                act.wait_ge(qk_projected[c], at_qk(t, a, g) + 1)
                if narrow(a):
                    if g == 0:
                        act.wait_ge(k_masked[c], at_masked(t, a, 0))
                    for i in range(2):
                        last = nc.scalar.activation(qk[c][:, 0, i * W:(i + 1) * W], bank(c, PROJ)[:, i * W:(i + 1) * W], ACT.Identity,
                                                    bias=small_part("qk_b")[:, 2 * a + i:2 * a + i + 1])
                else:
                    nc.scalar.copy(qk[c][:, g % 2, 0:W], bank(c, PROJ)[:, 0:W])
                    for h in range(2):
                        rows = slice(HALF * h, HALF * h + HALF)
                        last = nc.scalar.copy(k_head[c][rows, g % 2, h, :], bank(c, PROJ)[rows, W:2 * W])
                last.then_inc(qk_taken[c], 1)

            def take_v(t, c, a):
                act.wait_ge(v_projected[c], at_v(t, a, 1))
                src = bank(c, SCORE, 2).rearrange("p c (h d) -> p (c h) d", d=64)
                nc.scalar.copy(v64[c][:, 0, :, 0:64], src).then_inc(v_taken_act[c], 1)

            def exps(t, c, a, g):
                act.wait_ge(turned_ready[c], group(t, a, g) + 1)
                nc.scalar.activation(probsT[c][:, g % 2, :, :], bank(c, TURNED).rearrange("p (j n) -> p j n", j=J),
                                     ACT.Exp, scale=float(HEAD[a // 2]) ** -0.5).then_inc(probs_ready[c], 1)

            def take_oT(t, c, a, g):
                act.wait_ge(oT_turned[c], at_ot(t, a, g) + 1)
                nc.scalar.copy(oT[c][:, g, :, :], bank(c, PROJ)[:, 0:W].rearrange("p (b n) -> p b n", b=NB)
                               ).then_inc(oT_ready[c], 1)

            def mlp_block(t, c, layer, f):
                act.wait_ge(hidden_projected[c], t * LAYERS * F + layer * F + f + 1)
                at = (layer * 2 + GLU[layer]) * F + f
                bias = small_part("h_b")[:, at:at + 1]
                if GLU[layer]:
                    nc.scalar.activation(gate[c][:, f, :], bank(c, PROJ + f % 2)[:, W:2 * W], GELU[layer],
                                         bias=bias).then_inc(gate_ready[c], 1)
                else:
                    nc.scalar.activation(hidden[c][:, f, :], bank(c, PROJ + f % 2)[:, 0:W], GELU[layer],
                                         bias=bias).then_inc(hidden_ready[c], 1)

            def stream(t, c):
                act.wait_ge(ctx_taken[c], t + 1)
                nc.scalar.copy(ctxT[c][:], bank(c, SCORE)[0:CD, 0:W]).then_inc(ctxT_ready[c], 1)
                yield
                act.wait_ge(ctx_projected[c], t + 1)
                nc.scalar.activation(ctx_projT[c][:], bank(c, TURNED)[:, 0:W], ACT.Identity,
                                     bias=small_part("ctx_b")).then_inc(ctx_projT_ready[c], 1)
                act.wait_ge(normedT_ready[c], t * NORMS + 1)
                nc.scalar.activation(ctx_normT[c][:], bank(c, PROJ)[0:CD, 0:W], ACT.Identity,
                                     bias=small_part("ctx_ln_b")[0:CD],
                                     scale=small_part("ctx_ln_w")[0:CD]).then_inc(hT_ready[c], 1)
                yield
                for s in range(SUBS):
                    layer, kind = divmod(s, 3)
                    a = 2 * layer + kind
                    yield
                    modulate(t, c, s)
                    yield
                    if kind == 2:
                        for pair in range(2):
                            mlp_block(t, c, layer, 2 * pair)
                            mlp_block(t, c, layer, 2 * pair + 1)
                            yield
                        yield
                        continue
                    if not rotary(a):
                        if s == 6:
                            act.wait_ge(k_cleared[c], t + 1)
                        take_qk(t, c, a, 0)
                    if wide(a):
                        take_v(t, c, a)
                    yield
                    for i in range(G + LAGS):
                        if wide(a) and 0 <= i - 3 < G:
                            take_oT(t, c, a, i - 3)
                        if 0 <= i - 1 < G:
                            exps(t, c, a, i - 1)
                        if wide(a) and not rotary(a) and i + 1 < G:
                            take_qk(t, c, a, i + 1)
                        if narrow(a) and i == G + LAGS - 1:
                            take_oT(t, c, a, 0)
                        yield
                    yield
                act.wait_ge(out_ready[c], t + 1)
                act.dma_start(out[bass.ds(first_sequence(t, c), NB)].rearrange("b n d -> n b d"), x_out[c][:]
                              ).then_inc(stored[c], 16)
                yield

            with act.Fori(0, TURNS) as t:
                interleave(stream(t, 0), stream(t, 1))

        @block.vector
        def _(dve):
            dve.wait_ge(mod_projected, 1)
            dve.wait_ge(small_loaded, 16)
            nc.vector.tensor_tensor(mod_sum[:].rearrange("p s k b -> p (s k) b"),
                                    ps[:, 0, 0:2 * SUBS * B].rearrange("p (n b) -> p n b", b=B),
                                    small_part("mod_b").unsqueeze(2).to_broadcast([P, 2 * SUBS, B]),
                                    ALU.add).then_inc(mod_step, 1)
            dve.wait_ge(mod_step, 1)
            nc.vector.tensor_scalar(mod_gain[:], mod_sum[:, :, 0, :], 1.0, None, ALU.add).then_inc(mod_step, 1)
            dve.wait_ge(mod_step, 2)
            by_seq = mods[:].rearrange("p b s k -> p s k b")
            nc.vector.tensor_tensor(by_seq[:, :, 0, :], mod_gain[:],
                                    small_part("ln_w").unsqueeze(2).to_broadcast([P, SUBS, B]), ALU.mult).then_inc(mod_step, 1)
            nc.vector.tensor_tensor(mod_shift[:], mod_gain[:],
                                    small_part("ln_b").unsqueeze(2).to_broadcast([P, SUBS, B]), ALU.mult).then_inc(mod_step, 1)
            dve.wait_ge(mod_step, 4)
            nc.vector.tensor_tensor(by_seq[:, :, 1, :], mod_shift[:], mod_sum[:, :, 1, :], ALU.add).then_inc(mods_ready, 1)
            dve.wait_ge(mods_ready, 1)
            dve.wait_ge(consts_ready, 3 + 2 * STREAMS)

            def norm(t, c, n, src, width):
                for b in range(NB):
                    last = nc.vector.bn_stats(stats[c][:, b, :], src[:, b, :])
                last.then_inc(stats_ready[c], 1)
                dve.wait_ge(stats_ready[c], t * NORMS + n + 1)
                nc.vector.tensor_copy(wait_taker[:], stats[c][:, 0, 0:1])
                for b in range(NB):
                    last = nc.vector.bn_aggr(mean_var[c][:, b, :], stats[c][:, b, :])
                last.then_inc(mean_ready[c], 1)
                dve.wait_ge(mean_ready[c], t * NORMS + n + 1)
                dve.wait_ge(rstd_ready[c], t * NORMS + n + 1)
                for b in range(NB):
                    last = nc.vector.tensor_scalar(normed[c][:, b, 0:width], src[:, b, :], mean_var[c][:, b, 0:1],
                                                   rstd[c][:, b:b + 1], ALU.subtract, ALU.mult)
                last.then_inc(normed_ready[c], 1)

            def rotate(t, c, a, g):
                n = at_rotated(t, a, g)
                dve.wait_ge(qk_projected[c], at_qk(t, a, g) + 1)
                dve.wait_ge(qk_rotated[c], n)

                def table(name):
                    return small_part(name).unsqueeze(1).to_broadcast([P, 4, P])

                src = bank(c, PROJ)
                nc.vector.tensor_tensor(rot_a[c][:].rearrange("p (j n) -> p j n", n=P), src.rearrange("p (j n) -> p j n", n=P),
                                        table("cos"), ALU.mult).then_inc(rot_a_ready[c], 1)
                nc.vector.stream_shuffle(rot_swap[c][:], src, PAIR_SWAP).then_inc(qk_taken[c], 1)
                dve.wait_ge(qk_taken[c], at_qk(t, a, g) + 1)
                nc.vector.tensor_tensor(rot_b[c][:].rearrange("p (j n) -> p j n", n=P),
                                        rot_swap[c][:].rearrange("p (j n) -> p j n", n=P), table("sin"),
                                        ALU.mult).then_inc(rot_b_ready[c], 1)

            def take_v(t, c, a, part):
                dve.wait_ge(v_projected[c], at_v(t, a, part) + 1)
                if narrow(a):
                    at = (a if a < 2 else a - 4) * P
                    bias = small_part("v_b")[:, at:at + P].rearrange("p (h d) -> p h d", h=H)
                    nc.vector.tensor_tensor(v8[c][:, :, :, 0:8],
                                            bank(c, SCORE)[:, 0:W].rearrange("p (b h d) -> p b h d", b=NB, h=H),
                                            bias.unsqueeze(1).to_broadcast([P, NB, H, 8]), ALU.add).then_inc(v_taken_dve[c], 1)
                else:
                    src = bank(c, (OUT, TURNED)[part])
                    nc.vector.tensor_copy(v64[c][:, 1, 8 * part:8 * part + 8, 0:64],
                                          src.rearrange("p (h d) -> p h d", d=64)).then_inc(v_taken_dve[c], 1)

            def shift(t, c, a, g):
                n = group(t, a, g)
                dve.wait_ge(scores_ready[c], n + 1)
                scores = bank(c, SCORE).rearrange("p (j m) -> p j m", j=J)
                nc.vector.tensor_reduce(top[c][:, g % 2, :], scores, AX.X, ALU.max).then_inc(top_ready[c], 1)
                dve.wait_ge(top_ready[c], n + 1)
                nc.vector.tensor_tensor(shifted[c][:, g % 2, :, :], scores,
                                        top[c][:, g % 2, :].unsqueeze(2).to_broadcast([P, J, P]),
                                        ALU.subtract).then_inc(shifted_ready[c], 1)

            def normalise(t, c, a, g):
                n = group(t, a, g)
                d = HEAD[a // 2]
                dve.wait_ge(o_ready[c], n + 1)
                o = bank(c, OUT)[:, 0:J * (d + 1)].rearrange("p (j d) -> p j d", j=J)
                nc.vector.reciprocal(inv[c][:, g % 2, :], o[:, :, d]).then_inc(inv_ready[c], 1)
                dve.wait_ge(inv_ready[c], n + 1)
                dst = o8[c][:, :, 16 * g:16 * g + 16] if narrow(a) else o64[c][:, g % 2, :, :]
                nc.vector.tensor_tensor(dst.rearrange("p b (h d) -> p h b d", h=2),
                                        o[:, :, 0:d].rearrange("p (h b) d -> p h b d", h=2),
                                        inv[c][:, g % 2, :].rearrange("p (h b) -> p h b", h=2).unsqueeze(3)
                                        .to_broadcast([P, 2, NB, d]), ALU.mult).then_inc(o_normed[c], 1)

            def glu(t, c, layer, f):
                dve.wait_ge(gate_ready[c], t * F + f + 1)
                at = layer * 2 * F + f
                nc.vector.scalar_tensor_tensor(out=hidden[c][:, f, :], in0=bank(c, PROJ + f % 2)[:, 0:W],
                                               scalar=small_part("h_b")[:, at:at + 1], in1=gate[c][:, f, :],
                                               op0=ALU.add, op1=ALU.mult).then_inc(glu_ready[c], 1)

            def add_residual(t, c, s):
                dve.wait_ge(y_ready[c], t * SUBS + s + 1)
                dve.wait_ge(x_biased_ready[c], t * SUBS + s + 1)
                if s == SUBS - 1:
                    dve.wait_ge(stored[c], t * 16)
                    dst, done = x_out[c], out_ready[c]
                else:
                    dst, done = xs[c], x_ready[c]
                nc.vector.tensor_tensor(dst[:], bank(c, TURNED, 2)[:, :, 0:P], x_biased[c][:], ALU.add).then_inc(done, 1)

            def stream(t, c):
                dve.wait_ge(inputs_loaded[c], t * 32 + 32)
                each = NB * SUBS * 2
                nc.vector.tensor_copy(mod[c][:].rearrange("p b s k -> p (b s k)"),
                                      mods[:].rearrange("p b s k -> p (b s k)")[:, bass.ds((t * STREAMS + c) * each, each)]
                                      ).then_inc(mod_ready[c], 1)
                nc.vector.tensor_copy(xs[c][:], x_in[c][:]).then_inc(x_ready[c], 1)
                norm(t, c, 0, ctx_in[c], CD)
                yield
                yield
                for s in range(SUBS):
                    layer, kind = divmod(s, 3)
                    a = 2 * layer + kind
                    if s:
                        add_residual(t, c, s - 1)
                    else:
                        dve.wait_ge(normedT_ready[c], t * NORMS + 1)
                        dve.wait_ge(normed_ready[c], t * NORMS + 1)
                    dve.wait_ge(x_ready[c], t * SUBS + s + 1)
                    if s == 0:
                        nc.vector.tensor_copy(stats[c][:, 0, 0:1], mean_var[c][:, 0, 0:1]).then_inc(inputs_taken[c], 1)
                        dve.wait_ge(inputs_taken[c], t + 1)
                    norm(t, c, 1 + s, xs[c], P)
                    yield
                    yield
                    if kind == 2:
                        for pair in range(2):
                            if GLU[layer]:
                                glu(t, c, layer, 2 * pair)
                                glu(t, c, layer, 2 * pair + 1)
                            yield
                        yield
                        continue
                    take_v(t, c, a, 0)
                    if rotary(a):
                        rotate(t, c, a, 0)
                    yield
                    for i in range(G + LAGS):
                        if wide(a) and i == 0:
                            take_v(t, c, a, 1)
                        if i < G:
                            shift(t, c, a, i)
                        if 0 <= i - 2 < G:
                            normalise(t, c, a, i - 2)
                        if rotary(a) and i + 1 < G:
                            rotate(t, c, a, i + 1)
                        yield
                    yield
                add_residual(t, c, SUBS - 1)
                yield

            with dve.Fori(0, TURNS) as t:
                interleave(stream(t, 0), stream(t, 1))

        @block.tensor
        def _(pe):
            mm = nc.tensor.matmul
            pe.wait_ge(small_loaded, 16)
            pe.wait_ge(mod_w_loaded, 16)
            pe.wait_ge(silu_ready, 1)
            for n in range(2 * SUBS):
                src = cond_silu[:] if n // 6 in (0, 3) else small_part("cond")
                last = mm(ps[:, 0, n * B:(n + 1) * B], mod_w[:, n * P:(n + 1) * P], src, start=True, stop=True)
            last.then_inc(mod_projected, 1)

            def turn_norm(t, c, n, width):
                pe.wait_ge(normed_ready[c], t * NORMS + n + 1)
                for b in range(NB):
                    last = nc.tensor.transpose(bank(c, PROJ)[0:width, b * P:(b + 1) * P], normed[c][:, b, 0:width], ident)
                last.then_inc(normedT_ready[c], 1)

            def kv_source(c, a):
                if a % 2 == 0:
                    return hT[c], P
                return [(ctxT[c], CD), (ctx_normT[c], CD), (ctxT[c], CD), (ctx_projT[c], P)][a // 2]

            def project_qk(t, c, a, g):
                s, (kv, depth) = sub_of(a), kv_source(c, a)
                if g >= 4:
                    pe.wait_ge(oT_ready[c], at_ot(t, a, g - 3))
                if g:
                    pe.wait_ge(qk_taken[c], at_qk(t, a, g))
                cols = slice(g * P, (g + 1) * P)
                mm(bank(c, PROJ)[:, 0:W], weight(s, "q")[:, cols], hT[c][:], start=True, stop=True)
                mm(bank(c, PROJ)[:, W:2 * W], weight(s, "k")[0:depth, cols], kv[0:depth, :],
                   start=True, stop=True).then_inc(qk_projected[c], 1)

            def project_v(t, c, a, part):
                s, (kv, depth) = sub_of(a), kv_source(c, a)
                if narrow(a):
                    for b in range(NB):
                        last = mm(bank(c, SCORE)[:, b * P:(b + 1) * P], kv[0:depth, b * P:(b + 1) * P],
                                  weight(s, "v")[0:depth, :], start=True, stop=True)
                else:
                    for b, half, where in (((0, 0, SCORE), (0, 1, TURNED), (1, 0, OUT)), ((1, 1, TURNED),))[part]:
                        last = mm(bank(c, where), kv[0:depth, b * P:(b + 1) * P],
                                  weight(s, "v")[0:depth, half * 512:(half + 1) * 512], start=True, stop=True)
                last.then_inc(v_projected[c], 1)

            def scores(t, c, a, g):
                n = group(t, a, g)
                if masked(a):
                    pe.wait_ge(k_masked[c], at_masked(t, a, g) + 1)
                else:
                    pe.wait_ge(qk_taken[c], at_qk(t, a, g) + 1)
                if g == 0:
                    pe.wait_ge(v_taken_dve[c], at_v(t, a, 1))
                    if wide(a):
                        pe.wait_ge(v_taken_act[c], at_wide(t, a) + 1)
                else:
                    pe.wait_ge(shifted_ready[c], n)
                for h in range(2):
                    for b in range(NB):
                        j = NB * h + b
                        last = mm(bank(c, SCORE)[:, j * P:(j + 1) * P],
                                  qk[c][:, 0 if narrow(a) else g % 2, b * P:(b + 1) * P],
                                  k_head[c][:, g % 2, h, b * P:(b + 1) * P], start=True, stop=True)
                last.then_inc(scores_ready[c], 1)

            def turn_shifted(t, c, a, g):
                n = group(t, a, g)
                if g == 0:
                    pe.wait_ge(v_taken_dve[c], at_v(t, a, v_parts(a)))
                else:
                    pe.wait_ge(probs_ready[c], n)
                pe.wait_ge(shifted_ready[c], n + 1)
                for j in range(J):
                    last = nc.tensor.transpose(bank(c, TURNED)[:, j * P:(j + 1) * P], shifted[c][:, g % 2, j, :], ident)
                last.then_inc(turned_ready[c], 1)

            def apply_probs(t, c, a, g):
                n = group(t, a, g)
                d = HEAD[a // 2]
                v = (v8 if narrow(a) else v64)[c]
                if g:
                    pe.wait_ge(o_normed[c], n)
                pe.wait_ge(probs_ready[c], n + 1)
                for h in range(2):
                    for b in range(NB):
                        j = NB * h + b
                        last = mm(bank(c, OUT)[:, j * (d + 1):(j + 1) * (d + 1)], probsT[c][:, g % 2, j, :],
                                  v[:, b, 2 * g + h, :], start=True, stop=True)
                last.then_inc(o_ready[c], 1)

            def turn_back(t, c, a, g):
                if wide(a):
                    pe.wait_ge(qk_taken[c], at_qk(t, a, min(g + 4, G)))
                    if g:
                        pe.wait_ge(oT_ready[c], at_ot(t, a, g))
                pe.wait_ge(o_normed[c], group(t, a, G if narrow(a) else g + 1))
                for b in range(NB):
                    src = o8[c][:, b, :] if narrow(a) else o64[c][:, g % 2, b, :]
                    last = nc.tensor.transpose(bank(c, PROJ)[:, b * P:(b + 1) * P], src, ident)
                last.then_inc(oT_turned[c], 1)

            def project_out(t, c, a):
                blocks = ot_count(a)
                pe.wait_ge(oT_ready[c], at_ot(t, a, blocks))
                for b in range(NB):
                    for g in range(blocks):
                        last = mm(bank(c, TURNED + b)[:, 0:P], oT[c][:, g, b, :], weight(sub_of(a), "o")[:, g * P:(g + 1) * P],
                                  start=(g == 0), stop=(g == blocks - 1))
                last.then_inc(y_ready[c], 1)

            def mlp_up(t, c, layer, f):
                for i in range(2 if GLU[layer] else 1):
                    last = mm(bank(c, PROJ + f % 2)[:, i * W:(i + 1) * W],
                              weight(3 * layer + 2, "w1")[:, (i * F + f) * P:(i * F + f + 1) * P], hT[c][:], start=True, stop=True)
                last.then_inc(hidden_projected[c], 1)

            def mlp_down(t, c, layer, f):
                if GLU[layer]:
                    pe.wait_ge(glu_ready[c], t * F + f + 1)
                else:
                    done = F * sum(not GLU[i] for i in range(layer))
                    pe.wait_ge(hidden_ready[c], t * F * sum(not g for g in GLU) + done + f + 1)
                for b in range(NB):
                    last = mm(bank(c, TURNED + b)[:, 0:P], hidden[c][:, f, b * P:(b + 1) * P],
                              weight(3 * layer + 2, "w2")[:, f * P:(f + 1) * P], start=(f == 0), stop=(f == F - 1))
                if f == F - 1:
                    last.then_inc(y_ready[c], 1)

            def stream(t, c):
                pe.wait_ge(inputs_loaded[c], t * 32 + 32)
                for b in range(NB):
                    last = nc.tensor.transpose(bank(c, SCORE)[0:CD, b * P:(b + 1) * P], ctx_in[c][:, b, :], ident)
                last.then_inc(ctx_taken[c], 1)
                yield
                pe.wait_ge(ctxT_ready[c], t + 1)
                mm(bank(c, TURNED)[:, 0:W], small_part("ctx_w")[0:CD, :], ctxT[c][:], start=True, stop=True
                   ).then_inc(ctx_projected[c], 1)
                turn_norm(t, c, 0, CD)
                yield
                for s in range(SUBS):
                    layer, kind = divmod(s, 3)
                    a = 2 * layer + kind
                    yield
                    if s == 0:
                        pe.wait_ge(ctx_projT_ready[c], t + 1)
                        pe.wait_ge(hT_ready[c], t * NORMS + 1)
                    turn_norm(t, c, 1 + s, P)
                    yield
                    pe.wait_ge(weights_loaded[s], 16)
                    pe.wait_ge(hT_ready[c], t * NORMS + s + 2)
                    if kind == 2:
                        mlp_up(t, c, layer, 0)
                        mlp_up(t, c, layer, 1)
                        yield
                        for f in (0, 1):
                            mlp_down(t, c, layer, f)
                        for f in (2, 3):
                            mlp_up(t, c, layer, f)
                        yield
                        for f in (2, 3):
                            mlp_down(t, c, layer, f)
                        yield
                        continue
                    project_qk(t, c, a, 0)
                    project_v(t, c, a, 0)
                    yield
                    for i in range(G + LAGS):
                        if wide(a) and 0 <= i - 3 < G:
                            turn_back(t, c, a, i - 3)
                        if wide(a) and i == 0:
                            pe.wait_ge(v_taken_act[c], at_wide(t, a) + 1)
                            project_v(t, c, a, 1)
                        if i < G:
                            scores(t, c, a, i)
                        if 0 <= i - 1 < G:
                            turn_shifted(t, c, a, i - 1)
                        if 0 <= i - 2 < G:
                            apply_probs(t, c, a, i - 2)
                        if wide(a) and i + 1 < G:
                            project_qk(t, c, a, i + 1)
                        if narrow(a) and i == G + LAGS - 1:
                            turn_back(t, c, a, 0)
                        yield
                    project_out(t, c, a)
                    yield
                yield

            pe.wait_ge(mods_ready, 1)
            with pe.Fori(0, TURNS) as t:
                interleave(stream(t, 0), stream(t, 1))


def pack_weights(inputs):
    import numpy as np

    def rows(a):
        a = np.asarray(a)
        full = np.zeros((P, a.shape[1]), a.dtype)
        full[:a.shape[0]] = a
        return full

    def blocks(a):
        a = np.asarray(a)
        return a.reshape(-1, P, a.shape[1]).transpose(1, 0, 2).reshape(P, -1)

    L0, L1, L2, L3 = ({k[9:]: v for k, v in inputs.items() if k.startswith(f"L{i}_xcond_")} for i in range(4))
    q0, k0, v0 = np.split(np.asarray(L0["Wqkv"]), 3, axis=1)
    q3, k3, v3 = np.split(np.asarray(L3["W_qkv"]), 3, axis=1)
    sk, sv = np.split(np.asarray(L1["sa_wkv"]), 2, axis=1)
    ck, cv = np.split(np.asarray(L1["ca_wkv"]), 2, axis=1)
    parts = [
        [rows(q0), rows(k0), rows(v0), blocks(L0["Wos"])],
        [rows(L0["Wq"]), rows(L0["Wk"]), rows(L0["Wv"]), blocks(L0["Woc"])],
        [rows(L0["W1"]), blocks(L0["W2"])],
        [rows(L1["sa_wq"]), rows(sk), rows(sv), blocks(L1["sa_wo"])],
        [rows(L1["ca_wq"]), rows(ck), rows(cv), blocks(L1["ca_wo"])],
        [rows(L1["ff_w1"]), blocks(L1["ff_w2"])],
        [rows(L2["q1"]), rows(L2["k1"]), rows(L2["v1"]), blocks(L2["o1_w"])],
        [rows(L2["q2"]), rows(L2["k2"]), rows(L2["v2"]), blocks(L2["o2_w"])],
        [rows(L2["ff_w1"]), blocks(L2["ff_w2"])],
        [rows(q3), rows(k3), rows(v3), blocks(L3["W_proj"])],
        [rows(L3["W_q"]), rows(L3["W_k"]), rows(L3["W_v"]), blocks(L3["W_out"])],
        [rows(L3["W_fc1"]), blocks(L3["W_fc2"])],
    ]
    return [np.ascontiguousarray(np.concatenate(p, axis=1)) for p in parts]


def pack_small(inputs):
    import numpy as np

    L0, L1, L2, L3 = ({k[9:]: np.asarray(v) for k, v in inputs.items() if k.startswith(f"L{i}_xcond_")} for i in range(4))
    where, width = small_columns()
    full = np.zeros((P, width), np.float32)
    mod_w = np.zeros((P, 2 * SUBS * P), np.float32)

    def put(name, a, at=0):
        a = np.asarray(a)
        start = where[name][0] + at
        full[:a.shape[0], start:start + a.shape[1]] = a

    def cols(a):
        return np.asarray(a).reshape(-1, P).T

    def everywhere(a):
        return np.broadcast_to(np.asarray(a).reshape(1, -1), (P, np.asarray(a).size))

    put("ident", np.eye(P, dtype=np.float32))
    put("cond", np.asarray(inputs["cond_1024"]).T)
    m0, c0 = L0["Wmod"], L0["bmod"]
    m3, c3 = L3["W_ada"], L3["b_ada"]
    part = lambda a, i: a[..., i * P:(i + 1) * P]
    pairs = [(m0, c0, 1), (m0, c0, 0), (m0, c0, 3), (m0, c0, 2), (m0, c0, 5), (m0, c0, 4)]
    pairs += [(L1["g1_w"], L1["g1_b"], 0), (L1["b1_w"], L1["b1_b"], 0)] * 2
    pairs += [(L1["g2_w"], L1["g2_b"], 0), (L1["b2_w"], L1["b2_b"], 0)]
    for n in "123":
        pairs += [(L2[f"n{n}_w"], L2[f"n{n}_b"], 0), (L2[f"n{n}_w"], L2[f"n{n}_b"], 1)]
    pairs += [(m3, c3, 1), (m3, c3, 0), (m3, c3, 3), (m3, c3, 2), (m3, c3, 5), (m3, c3, 4)]
    for n, (w, b, i) in enumerate(pairs):
        mod_w[:, n * P:(n + 1) * P] = part(w, i)
        put("mod_b", cols(part(b, i)), n)
    norms = [("ln1", L0), ("ln2", L0), ("ln3", L0), ("ln1", L1), ("ln1", L1), ("ln2", L1)]
    for s in range(SUBS):
        if s < len(norms):
            name, layer = norms[s]
            put("ln_w", cols(layer[name + "_w"]), s)
            put("ln_b", cols(layer[name + "_b"]), s)
        else:
            put("ln_w", np.ones((P, 1), np.float32), s)
    put("ctx_w", L3["W_ctx"])
    put("ctx_b", cols(L3["b_ctx"]))
    put("ctx_ln_w", L1["ca_lnc_w"].reshape(CD, 1))
    put("ctx_ln_b", L1["ca_lnc_b"].reshape(CD, 1))
    d = 64
    inv_freq = np.float32(1.0) / np.float32(10000.0) ** (np.arange(0, d, 2, dtype=np.float32) / np.float32(d))
    angle = np.arange(P, dtype=np.float32)[None, :] * inv_freq[:, None]
    put("cos", np.tile(np.repeat(np.cos(angle), 2, axis=0), (2, 1)))
    put("sin", np.tile(np.stack([-np.sin(angle), np.sin(angle)], axis=1).reshape(d, P), (2, 1)))

    put("half_mask", np.repeat(np.eye(2, dtype=np.float32), HALF, axis=0))
    put("head_mask", np.repeat(np.eye(H, dtype=np.float32), P // H, axis=0))

    bq0, bk0, bv0 = np.split(L0["bqkv"], 3)
    bq3, bk3, bv3 = np.split(L3["b_qkv"], 3)
    for a, (bq, bk, bv) in {0: (bq0, bk0, bv0), 1: (L0["bq"], L0["bk"], L0["bv"]), 6: (bq3, bk3, bv3)}.items():
        put("qk_b", cols(bq), 2 * a)
        put("qk_b", cols(bk), 2 * a + 1)
        put("v_b", everywhere(bv), (a if a < 2 else a - 4) * P)
    outs = [L0["bos"], L0["boc"], L0["b2"], L1["sa_bo"], L1["ca_bo"], L1["ff_b2"],
            L2["o1_b"], L2["o2_b"], L2["ff_b2"], L3["b_proj"], L3["b_out"], L3["b_fc2"]]
    for s, b in enumerate(outs):
        put("out_b", everywhere(b), s * P)
    for layer, b in enumerate([L0["b1"], L1["ff_b1"], L2["ff_b1"], L3["b_fc1"]]):
        put("h_b", cols(b), layer * 2 * F)
    return full, mod_w


def kernel(**inputs):
    import numpy as np
    from concourse import bacc
    from concourse.bass_utils import run_bass_kernel_spmd

    arrays = {
        "x_dram": np.ascontiguousarray(inputs["x"]),
        "ctx_dram": np.ascontiguousarray(inputs["ctx_768"]),
    }
    arrays["small_dram"], arrays["mod_w_dram"] = pack_small(inputs)
    for s, w in enumerate(pack_weights(inputs)):
        arrays[f"weights{s}_dram"] = w
    nc = bacc.Bacc("TRN2", target_bir_lowering=False, num_devices=1)
    aps = {n: nc.dram_tensor(n, a.shape, mybir.dt.from_np(a.dtype), kind="ExternalInput").ap() for n, a in arrays.items()}
    out = nc.dram_tensor("out_dram", (B, P, P), F32, kind="ExternalOutput").ap()
    build(nc, aps["x_dram"], aps["ctx_dram"], aps["small_dram"], aps["mod_w_dram"],
          [aps[f"weights{s}_dram"] for s in range(SUBS)], out)
    r = run_bass_kernel_spmd(nc, [arrays], core_ids=[0])
    return r.results[0]["out_dram"]
```

```python
from contextlib import ExitStack

import concourse.bass as bass
from concourse import mybir

ALU = mybir.AluOpType
ACT = mybir.ActivationFunctionType
AX = mybir.AxisListType
F32 = mybir.dt.float32

P = 128
B = 8
NB = 2
STREAMS = 2
TURNS = B // (NB * STREAMS)
W = NB * P
CD = 96
H = 16
G = 8
J = 2 * NB
LAYERS = 4
SUBS = 3 * LAYERS
ATT = 2 * LAYERS
F = 4
V_ROWS = 32
HALF = 64

HEAD = [8, 64, 64, 8]
ROPE = [False, True, False, False]
GLU = [False, False, True, False]
EPS = [1e-5, 1e-5, 1e-5, 1e-6]
GELU = [ACT.Gelu, ACT.Gelu, ACT.Gelu, ACT.Gelu_apprx_tanh]
PAIR_SWAP = [i ^ 1 for i in range(32)]

CONTEXT_STEPS = 2
NORM_STEPS = 2
AHEAD = 2
LAGS = 3
ATTENTION_STEPS = 1 + G + LAGS + 1
NARROW_STEPS = ATTENTION_STEPS + 1
MLP_STEPS = 3
STEPS = 2 * sum(NARROW_STEPS if d == 8 else ATTENTION_STEPS for d in HEAD) + CONTEXT_STEPS + LAYERS * (3 * NORM_STEPS + MLP_STEPS) + 1
BEHIND = 5


def interleave(first, second):
    for n in range(STEPS + BEHIND):
        if n < STEPS:
            next(first)
        if n >= BEHIND:
            next(second)
    assert next(first, None) is None and next(second, None) is None


def narrow(a):
    return HEAD[a // 2] == 8


def sub_of(a):
    return 3 * (a // 2) + a % 2


def weight_columns(s):
    layer, kind = divmod(s, 3)
    if kind == 2:
        parts = [("w1", F * P * (2 if GLU[layer] else 1)), ("w2", F * P)]
    else:
        width = H * HEAD[layer]
        parts = [("q", width), ("k", width), ("v", width), ("o", width)]
    at, where = 0, {}
    for name, width in parts:
        where[name] = (at, width)
        at += width
    return where, at


def small_columns():
    parts = [("ident", P), ("cond", B), ("mod_b", 2 * SUBS), ("ln_w", SUBS), ("ln_b", SUBS),
             ("ctx_w", P), ("ctx_b", 1), ("ctx_ln_w", 1), ("ctx_ln_b", 1), ("cos", P), ("sin", P), ("head_mask", H),
             ("qk_b", 2 * ATT), ("v_b", 4 * P), ("out_b", SUBS * P), ("h_b", LAYERS * 2 * F)]
    at, where = 0, {}
    for name, width in parts:
        where[name] = (at, width)
        at += width
    return where, at


def build(nc, x, ctx, small, mod_weights, weights, out):
    s_at, s_width = small_columns()
    w_at = [weight_columns(s) for s in range(SUBS)]

    with ExitStack() as stack:
        def sb(name, shape):
            return stack.enter_context(nc.sbuf_tensor(name, shape, F32))

        def sem(name):
            return stack.enter_context(nc.semaphore(name))

        def sb2(name, shape):
            return [sb(f"{name}_{c}", shape) for c in range(STREAMS)]

        def sem2(name):
            return [sem(f"{name}_{c}") for c in range(STREAMS)]

        sm = sb("small_sb", [P, s_width])
        w_sb = [sb(f"w_sb{s}", [P, w_at[s][1]]) for s in range(SUBS)]

        def small_part(name):
            a, n = s_at[name]
            return sm[:, a:a + n]

        def weight(s, name):
            a, n = w_at[s][0][name]
            return w_sb[s][:, a:a + n]

        ident = small_part("ident")
        MOD_HOME = 3
        mod_w = w_sb[MOD_HOME][:, 0:2 * SUBS * P]
        cond_silu = sb("cond_silu", [P, B])
        mod_sum = sb("mod_sum", [P, SUBS, 2, B])
        mod_gain = sb("mod_gain", [P, SUBS, B])
        mod_shift = sb("mod_shift", [P, SUBS, B])
        mods = sb("mods", [P, B, SUBS, 2])
        minus_half = sb("minus_half", [P, NB])
        epsilon = sb("epsilon", [P, 2 * NB])
        wait_taker = sb("wait_taker", [P, 1])
        pool_wait_taker = sb("pool_wait_taker", [P, NB])
        mod = sb2("mod", [P, NB, SUBS, 2])
        x_in = sb2("x_in", [P, NB, P])
        ctx_in = sb2("ctx_in", [P, NB, CD])
        xs = sb2("xs", [P, NB, P])
        x_biased = sb2("x_biased", [P, NB, P])
        x_out = sb2("x_out", [P, NB, P])
        stats = sb2("stats", [P, NB, 6])
        mean_var = sb2("mean_var", [P, NB, 2])
        var_eps = sb2("var_eps", [P, NB])
        rstd = sb2("rstd", [P, NB])
        normed = sb2("normed", [P, NB, P])
        hT = sb2("hT", [P, W])
        ctxT = sb2("ctxT", [CD, W])
        ctx_normT = sb2("ctx_normT", [CD, W])
        ctx_projT = sb2("ctx_projT", [P, W])
        qk = sb2("qk", [P, 2, 2 * W])
        k_head = sb2("k_head", [P, 2, 2, W])
        rot_a = sb2("rot_a", [P, 2 * W])
        rot_products = sb2("rot_products", [P, 2, 2 * W])
        rot_swap = [r[:, 0, :] for r in rot_products]
        rot_b = [r[:, 1, :] for r in rot_products]
        v64 = sb2("v64", [P, NB, H, 65])
        v8 = [r.rearrange("p i c -> p (i c)").rearrange("p (b h d) -> p b h d", b=NB, h=H) for r in rot_products]
        o8T = [r[:, 0:2 * P].rearrange("p (i n) -> p i n", i=2) for r in rot_a]
        top = sb2("top", [P, 2, J])
        shifted = sb2("shifted", [P, 2, J, P])
        probsT = sb2("probsT", [P, 2, J, P])
        inv = sb2("inv", [P, 2, J])
        o64 = sb2("o64", [P, 2, NB, P])
        o8 = sb2("o8", [P, NB, P])
        oT = sb2("oT", [P, G, NB, P])
        hidden = [o[:].rearrange("p g b n -> p g (b n)")[:, 0:F, :] for o in oT]
        gate = [o[:].rearrange("p g b n -> p g (b n)")[:, F:2 * F, :] for o in oT]

        ps = stack.enter_context(nc.psum_tensor("ps", [P, 8, 512], F32))
        BANKS = 4
        PROJ, SCORE, TURNED, OUT = range(BANKS)

        MOD_BANK = 2 * BANKS - 1

        def bank(c, n, count=None):
            return ps[:, BANKS * c + n, :] if count is None else ps[:, BANKS * c + n:BANKS * c + n + count, :]

        small_loaded = sem("small_loaded")
        mod_w_loaded = sem("mod_w_loaded")
        weights_loaded = [sem(f"weights_loaded{s}") for s in range(SUBS)]
        consts_ready = sem("consts_ready")
        silu_ready = sem("silu_ready")
        mod_projected = sem("mod_projected")
        mod_step = sem("mod_step")
        mods_ready = sem("mods_ready")
        inputs_loaded = sem2("inputs_loaded")
        inputs_taken = sem2("inputs_taken")
        ctx_taken = sem2("ctx_taken")
        mod_ready = sem2("mod_ready")
        x_ready = sem2("x_ready")
        stats_ready = sem2("stats_ready")
        mean_ready = sem2("mean_ready")
        var_eps_ready = sem2("var_eps_ready")
        rstd_ready = sem2("rstd_ready")
        normed_ready = sem2("normed_ready")
        normedT_ready = sem2("normedT_ready")
        hT_ready = sem2("hT_ready")
        ctxT_ready = sem2("ctxT_ready")
        ctx_projected = sem2("ctx_projected")
        ctx_projT_ready = sem2("ctx_projT_ready")
        qk_projected = sem2("qk_projected")
        qk_taken = sem2("qk_taken")
        rot_a_ready = sem2("rot_a_ready")
        rot_b_ready = sem2("rot_b_ready")
        k_cleared = sem2("k_cleared")
        ones_restored = sem2("ones_restored")
        k_masked = sem2("k_masked")
        k_split = sem2("k_split")
        qk_rotated = sem2("qk_rotated")
        v_projected = sem2("v_projected")
        v_taken_act = sem2("v_taken_act")
        v_taken_dve = sem2("v_taken_dve")
        scores_ready = sem2("scores_ready")
        top_ready = sem2("top_ready")
        shifted_ready = sem2("shifted_ready")
        turned_ready = sem2("turned_ready")
        probs_ready = sem2("probs_ready")
        o_ready = sem2("o_ready")
        inv_ready = sem2("inv_ready")
        o_normed = sem2("o_normed")
        o8T_ready = sem2("o8T_ready")
        o8_turned = sem2("o8_turned")
        oT_turned = sem2("oT_turned")
        oT_ready = sem2("oT_ready")
        hidden_projected = sem2("hidden_projected")
        gate_ready = sem2("gate_ready")
        hidden_ready = sem2("hidden_ready")
        glu_ready = sem2("glu_ready")
        y_ready = sem2("y_ready")
        x_biased_ready = sem2("x_biased_ready")
        out_ready = sem2("out_ready")
        stored = sem2("stored")

        NORMS = SUBS + 1
        NG = ATT * G

        def before(a, kind, each):
            return each * sum(kind(i) for i in range(a))

        def rotary(a):
            return ROPE[a // 2]

        def wide(a):
            return not narrow(a)

        def qk_count(a):
            return 1 if narrow(a) else G

        def ot_count(a):
            return 1 if narrow(a) else G

        def v_parts(a):
            return 1 if narrow(a) else 2

        def group(t, a, g):
            return t * NG + a * G + g

        def at_rotated(t, a, g):
            return t * before(ATT, rotary, G) + before(a, rotary, G) + g

        def at_narrow(t, a, g):
            return t * before(ATT, narrow, G) + before(a, narrow, G) + g

        def at_qk(t, a, g):
            return t * before(ATT, qk_count, 1) + before(a, qk_count, 1) + g

        def at_ot(t, a, g):
            return t * before(ATT, ot_count, 1) + before(a, ot_count, 1) + g

        def at_v(t, a, n):
            return t * before(ATT, v_parts, 1) + before(a, v_parts, 1) + n

        def at_wide(t, a):
            return t * before(ATT, wide, 1) + before(a, wide, 1)

        def first_sequence(t, c):
            return (t * STREAMS + c) * NB

        block = stack.enter_context(nc.Block())

        @block.sync
        def _(sp):
            sp.dma_start(sm[:], small).then_inc(small_loaded, 16)
            sp.dma_start(mod_w, mod_weights).then_inc(mod_w_loaded, 16)

            def load(t, c):
                for dst, src in ((x_in[c], x), (ctx_in[c], ctx)):
                    sp.dma_start(dst[:], src[bass.ds(first_sequence(t, c), NB)].rearrange("b n d -> n b d")
                                 ).then_inc(inputs_loaded[c], 16)

            for c in range(STREAMS):
                load(0, c)
            with sp.Fori(1, TURNS) as t:
                for c in range(STREAMS):
                    sp.wait_ge(inputs_taken[c], t)
                    sp.wait_ge(ctx_taken[c], t)
                    load(t, c)
            for c in range(STREAMS):
                sp.wait_ge(stored[c], 16 + 16 * TURNS)

        @block.gpsimd
        def _(pool):
            nc.gpsimd.memset(minus_half[:], -0.5).then_inc(consts_ready, 1)
            nc.gpsimd.memset(epsilon[:, 0:NB], EPS[0]).then_inc(consts_ready, 1)
            nc.gpsimd.memset(epsilon[:, NB:2 * NB], EPS[LAYERS - 1]).then_inc(consts_ready, 1)
            for c in range(STREAMS):
                nc.gpsimd.memset(v64[c][:], 1.0).then_inc(consts_ready, 1)
                nc.gpsimd.memset(v8[c], 1.0).then_inc(consts_ready, 1)
                nc.gpsimd.memset(x_out[c][:], 0.0).then_inc(stored[c], 16)
            pool.wait_ge(consts_ready, 3 + 2 * STREAMS)
            pool.wait_ge(small_loaded, 16)

            def norm_scale(t, c, n, layer):
                at = NB if EPS[layer] != EPS[0] else 0
                pool.wait_ge(mean_ready[c], t * NORMS + n + 1)
                nc.gpsimd.tensor_tensor(var_eps[c][:], mean_var[c][:, :, 1], epsilon[:, at:at + NB],
                                        ALU.add).then_inc(var_eps_ready[c], 1)
                pool.wait_ge(var_eps_ready[c], t * NORMS + n + 1)
                nc.gpsimd.tensor_tensor(rstd[c][:], var_eps[c][:], minus_half[:], ALU.pow).then_inc(rstd_ready[c], 1)

            def add_bias(t, c, s):
                pool.wait_ge(x_ready[c], (t * SUBS + s + 1) * NB)
                bias = small_part("out_b")[:, s * P:(s + 1) * P]
                nc.gpsimd.tensor_tensor(x_biased[c][:], xs[c][:], bias.unsqueeze(1).to_broadcast([P, NB, P]),
                                        ALU.add).then_inc(x_biased_ready[c], 1)

            def clear_k(t, c):
                pool.wait_ge(scores_ready[c], group(t, 2, 0))
                some = ident.unsqueeze(1).to_broadcast([P, 2 * 2 * NB, P])
                nc.gpsimd.tensor_tensor(k_head[c][:].rearrange("p i h (b n) -> p (i h b) n", b=NB), some, some,
                                        ALU.subtract).then_inc(k_cleared[c], 1)

            def restore_ones(t, c):
                pool.wait_ge(scores_ready[c], group(t, 4, 0) + 1)
                nc.gpsimd.tensor_tensor(pool_wait_taker[:], minus_half[:], minus_half[:], ALU.add)
                nc.gpsimd.memset(rot_products[c][:], 1.0).then_inc(ones_restored[c], 1)

            def mask_k(t, c, a, g):
                if g >= 2:
                    pool.wait_ge(scores_ready[c], group(t, a, g - 1))
                pool.wait_ge(qk_taken[c], at_qk(t, a, 1))
                mask, k = small_part("head_mask")[:, 2 * g:2 * g + 2], qk[c][:, 0, W:2 * W]
                nc.gpsimd.tensor_tensor(k_head[c][:, g % 2, :, :], k.unsqueeze(1).to_broadcast([P, 2, W]),
                                        mask.unsqueeze(2).to_broadcast([P, 2, W]), ALU.mult).then_inc(k_masked[c], 1)

            def rotate(t, c, a, g):
                pool.wait_ge(rot_b_ready[c], at_rotated(t, a, g) + 1)
                nc.gpsimd.tensor_tensor(qk[c][:, g % 2, :], rot_a[c][:], rot_b[c], ALU.add).then_inc(qk_rotated[c], 1)

            def stream(t, c):
                norm_scale(t, c, 0, 1)
                yield
                yield
                for s in range(SUBS):
                    layer, kind = divmod(s, 3)
                    a = 2 * layer + kind
                    norm_scale(t, c, 1 + s, layer)
                    yield
                    if s == 3:
                        clear_k(t, c)
                    yield
                    if kind == 2:
                        add_bias(t, c, s)
                        for _ in range(MLP_STEPS):
                            yield
                        continue
                    if narrow(a):
                        for g in range(2):
                            mask_k(t, c, a, g)
                    if rotary(a):
                        rotate(t, c, a, 0)
                    yield
                    for i in range(G + LAGS + 1 + narrow(a)):
                        if narrow(a) and i + 2 < G:
                            mask_k(t, c, a, i + 2)
                        if i == G:
                            add_bias(t, c, s)
                        if a == 4 and i == 0:
                            restore_ones(t, c)
                        if rotary(a) and i + 1 < G:
                            rotate(t, c, a, i + 1)
                        yield
                yield

            with pool.Fori(0, TURNS) as t:
                interleave(stream(t, 0), stream(t, 1))

        @block.scalar
        def _(act):
            act.wait_ge(small_loaded, 16)
            nc.scalar.activation(cond_silu[:], small_part("cond"), ACT.Silu).then_inc(silu_ready, 1)
            for s in range(SUBS):
                if s == MOD_HOME:
                    act.wait_ge(mod_projected, 1)
                act.dma_start(w_sb[s][:], weights[s]).then_inc(weights_loaded[s], 16)
            act.wait_ge(silu_ready, 1)

            def modulate(t, c, s):
                act.wait_ge(mod_ready[c], t + 1)
                for b in range(NB):
                    act.wait_ge(normedT_ready[c], (t * NORMS + s + 1) * NB + b + 1)
                    last = nc.scalar.activation(hT[c][:, b * P:(b + 1) * P], bank(c, PROJ + b)[:, 0:P], ACT.Identity,
                                                bias=mod[c][:, b, s, 1:2], scale=mod[c][:, b, s, 0:1])
                last.then_inc(hT_ready[c], 1)

            def take_qk(t, c, a, g):
                act.wait_ge(qk_projected[c], at_qk(t, a, g) + 1)
                if narrow(a):
                    if a:
                        act.wait_ge(k_masked[c], at_narrow(t, a, 0))
                    for i in (1, 0):
                        last = nc.scalar.activation(qk[c][:, 0, i * W:(i + 1) * W], bank(c, PROJ)[:, i * W:(i + 1) * W], ACT.Identity,
                                                    bias=small_part("qk_b")[:, 2 * a + i:2 * a + i + 1])
                else:
                    nc.scalar.copy(qk[c][:, g % 2, 0:W], bank(c, PROJ)[:, 0:W])
                    last = split_k(c, g, bank(c, PROJ)[:, W:2 * W])
                last.then_inc(qk_taken[c], 1)

            def split_k(c, g, k):
                for h in range(2):
                    rows = slice(HALF * h, HALF * h + HALF)
                    last = nc.scalar.copy(k_head[c][rows, g % 2, h, :], k[rows])
                return last

            def take_rotated_k(t, c, a, g):
                if a == 2 and g == 0:
                    act.wait_ge(k_cleared[c], t + 1)
                act.wait_ge(qk_rotated[c], at_rotated(t, a, g) + 1)
                split_k(c, g, qk[c][:, g % 2, W:2 * W]).then_inc(k_split[c], 1)

            def take_v(t, c, a):
                act.wait_ge(v_projected[c], at_v(t, a, 1))
                src = bank(c, SCORE, 2).rearrange("p c (h d) -> p (c h) d", d=64)
                nc.scalar.copy(v64[c][:, 0, :, 0:64], src).then_inc(v_taken_act[c], 1)

            def exps(t, c, a, g):
                act.wait_ge(turned_ready[c], group(t, a, g) + 1)
                nc.scalar.activation(probsT[c][:, g % 2, :, :], bank(c, TURNED).rearrange("p (j n) -> p j n", j=J),
                                     ACT.Exp, scale=float(HEAD[a // 2]) ** -0.5).then_inc(probs_ready[c], 1)

            def take_o8T(t, c, a, g):
                act.wait_ge(o_ready[c], group(t, a, g) + 1)
                nc.scalar.copy(o8T[c][:, g % 2, :], bank(c, OUT)[:, 0:P]).then_inc(o8T_ready[c], 1)

            def take_oT(t, c, a, g):
                act.wait_ge(oT_turned[c], at_ot(t, a, g) + 1)
                nc.scalar.copy(oT[c][:, g, :, :], bank(c, PROJ)[:, 0:W].rearrange("p (b n) -> p b n", b=NB)
                               ).then_inc(oT_ready[c], 1)

            def mlp_block(t, c, layer, f):
                act.wait_ge(hidden_projected[c], t * LAYERS * F + layer * F + f + 1)
                at = (layer * 2 + GLU[layer]) * F + f
                bias = small_part("h_b")[:, at:at + 1]
                if GLU[layer]:
                    nc.scalar.activation(gate[c][:, f, :], bank(c, PROJ + f % 2)[:, W:2 * W], GELU[layer],
                                         bias=bias).then_inc(gate_ready[c], 1)
                else:
                    nc.scalar.activation(hidden[c][:, f, :], bank(c, PROJ + f % 2)[:, 0:W], GELU[layer],
                                         bias=bias).then_inc(hidden_ready[c], 1)

            def stream(t, c):
                act.wait_ge(ctx_taken[c], t + 1)
                nc.scalar.copy(ctxT[c][:], bank(c, SCORE)[0:CD, 0:W]).then_inc(ctxT_ready[c], 1)
                yield
                act.wait_ge(ctx_projected[c], t + 1)
                nc.scalar.activation(ctx_projT[c][:], bank(c, TURNED)[:, 0:W], ACT.Identity,
                                     bias=small_part("ctx_b")).then_inc(ctx_projT_ready[c], 1)
                act.wait_ge(normedT_ready[c], (t * NORMS + 1) * NB)
                nc.scalar.activation(ctx_normT[c][:].rearrange("p (b n) -> p b n", b=NB), bank(c, PROJ, NB)[0:CD, :, 0:P],
                                     ACT.Identity, bias=small_part("ctx_ln_b")[0:CD],
                                     scale=small_part("ctx_ln_w")[0:CD]).then_inc(hT_ready[c], 1)
                yield
                for s in range(SUBS):
                    layer, kind = divmod(s, 3)
                    a = 2 * layer + kind
                    yield
                    modulate(t, c, s)
                    yield
                    if kind == 2:
                        for pair in range(2):
                            mlp_block(t, c, layer, 2 * pair)
                            mlp_block(t, c, layer, 2 * pair + 1)
                            yield
                        yield
                        continue
                    if not rotary(a):
                        take_qk(t, c, a, 0)
                    if wide(a):
                        take_v(t, c, a)
                        if rotary(a):
                            take_rotated_k(t, c, a, 0)
                    yield
                    for i in range(G + LAGS):
                        if narrow(a) and 0 <= i - 3 <= G - 3:
                            take_o8T(t, c, a, i - 3)
                        if wide(a) and not rotary(a) and i + 1 < G:
                            take_qk(t, c, a, i + 1)
                        if 0 <= i - 1 < G:
                            exps(t, c, a, i - 1)
                        if wide(a) and 0 <= i - 3 < G:
                            take_oT(t, c, a, i - 3)
                        if rotary(a) and i + 1 < G:
                            take_rotated_k(t, c, a, i + 1)
                        if narrow(a) and G <= i < G + 2:
                            take_o8T(t, c, a, i - 2)
                        yield
                    if narrow(a):
                        take_oT(t, c, a, 0)
                        yield
                    yield
                act.wait_ge(out_ready[c], (t + 1) * NB)
                act.dma_start(out[bass.ds(first_sequence(t, c), NB)].rearrange("b n d -> n b d"), x_out[c][:]
                              ).then_inc(stored[c], 16)
                yield

            with act.Fori(0, TURNS) as t:
                interleave(stream(t, 0), stream(t, 1))

        @block.vector
        def _(dve):
            dve.wait_ge(mod_projected, 1)
            dve.wait_ge(small_loaded, 16)
            nc.vector.tensor_tensor(mod_sum[:].rearrange("p s k b -> p (s k) b"),
                                    ps[:, MOD_BANK, 0:2 * SUBS * B].rearrange("p (n b) -> p n b", b=B),
                                    small_part("mod_b").unsqueeze(2).to_broadcast([P, 2 * SUBS, B]),
                                    ALU.add).then_inc(mod_step, 1)
            dve.wait_ge(mod_step, 1)
            nc.vector.tensor_scalar(mod_gain[:], mod_sum[:, :, 0, :], 1.0, None, ALU.add).then_inc(mod_step, 1)
            dve.wait_ge(mod_step, 2)
            by_seq = mods[:].rearrange("p b s k -> p s k b")
            nc.vector.tensor_tensor(by_seq[:, :, 0, :], mod_gain[:],
                                    small_part("ln_w").unsqueeze(2).to_broadcast([P, SUBS, B]), ALU.mult).then_inc(mod_step, 1)
            nc.vector.tensor_tensor(mod_shift[:], mod_gain[:],
                                    small_part("ln_b").unsqueeze(2).to_broadcast([P, SUBS, B]), ALU.mult).then_inc(mod_step, 1)
            dve.wait_ge(mod_step, 4)
            nc.vector.tensor_tensor(by_seq[:, :, 1, :], mod_shift[:], mod_sum[:, :, 1, :], ALU.add).then_inc(mods_ready, 1)
            dve.wait_ge(mods_ready, 1)
            dve.wait_ge(consts_ready, 3 + 2 * STREAMS)

            def take_stats(t, c, n, src, s=0):
                for b in range(NB):
                    if s:
                        add_residual(t, c, s - 1, b)
                        dve.wait_ge(x_ready[c], (t * SUBS + s) * NB + b + 1)
                    last = nc.vector.bn_stats(stats[c][:, b, :], src[:, b, :])
                last.then_inc(stats_ready[c], 1)
                dve.wait_ge(stats_ready[c], t * NORMS + n + 1)
                nc.vector.tensor_copy(wait_taker[:], stats[c][:, 0, 0:1])
                for b in range(NB):
                    last = nc.vector.bn_aggr(mean_var[c][:, b, :], stats[c][:, b, :])
                last.then_inc(mean_ready[c], 1)

            def norm(t, c, n, src, width):
                dve.wait_ge(mean_ready[c], t * NORMS + n + 1)
                dve.wait_ge(rstd_ready[c], t * NORMS + n + 1)
                for b in range(NB):
                    nc.vector.tensor_scalar(normed[c][:, b, 0:width], src[:, b, :], mean_var[c][:, b, 0:1],
                                            rstd[c][:, b:b + 1], ALU.subtract, ALU.mult).then_inc(normed_ready[c], 1)

            def rotate(t, c, a, g):
                n = at_rotated(t, a, g)
                dve.wait_ge(qk_projected[c], at_qk(t, a, g) + 1)
                if a > 2 or g:
                    dve.wait_ge(qk_rotated[c], n)

                def table(name):
                    return small_part(name).unsqueeze(1).to_broadcast([P, 4, P])

                src = bank(c, PROJ)
                nc.vector.tensor_tensor(rot_a[c][:].rearrange("p (j n) -> p j n", n=P), src.rearrange("p (j n) -> p j n", n=P),
                                        table("cos"), ALU.mult).then_inc(rot_a_ready[c], 1)
                nc.vector.stream_shuffle(rot_swap[c], src, PAIR_SWAP).then_inc(qk_taken[c], 1)
                dve.wait_ge(qk_taken[c], at_qk(t, a, g) + 1)
                nc.vector.tensor_tensor(rot_b[c].rearrange("p (j n) -> p j n", n=P),
                                        rot_swap[c].rearrange("p (j n) -> p j n", n=P), table("sin"),
                                        ALU.mult).then_inc(rot_b_ready[c], 1)

            def take_v(t, c, a, part):
                dve.wait_ge(v_projected[c], at_v(t, a, part) + 1)
                if narrow(a):
                    if a == 6:
                        dve.wait_ge(ones_restored[c], t + 1)
                    at = (a if a < 2 else a - 4) * P
                    bias = small_part("v_b")[:, at:at + P].rearrange("p (h d) -> p h d", h=H)
                    nc.vector.tensor_tensor(v8[c][:, :, :, 0:8],
                                            bank(c, SCORE)[:, 0:W].rearrange("p (b h d) -> p b h d", b=NB, h=H),
                                            bias.unsqueeze(1).to_broadcast([P, NB, H, 8]), ALU.add).then_inc(v_taken_dve[c], 1)
                else:
                    src = bank(c, (OUT, TURNED)[part])
                    nc.vector.tensor_copy(v64[c][:, 1, 8 * part:8 * part + 8, 0:64],
                                          src.rearrange("p (h d) -> p h d", d=64)).then_inc(v_taken_dve[c], 1)

            def shift(t, c, a, g):
                n = group(t, a, g)
                dve.wait_ge(scores_ready[c], n + 1)
                scores = bank(c, SCORE).rearrange("p (j m) -> p j m", j=J)
                nc.vector.tensor_reduce(top[c][:, g % 2, :], scores, AX.X, ALU.max).then_inc(top_ready[c], 1)
                dve.wait_ge(top_ready[c], n + 1)
                nc.vector.tensor_tensor(shifted[c][:, g % 2, :, :], scores,
                                        top[c][:, g % 2, :].unsqueeze(2).to_broadcast([P, J, P]),
                                        ALU.subtract).then_inc(shifted_ready[c], 1)

            def normalise(t, c, a, g):
                n = group(t, a, g)
                d = HEAD[a // 2]
                if narrow(a):
                    dve.wait_ge(o8_turned[c], at_narrow(t, a, g) + 1)
                    o = bank(c, PROJ)[:, 0:J * V_ROWS].rearrange("p (j d) -> p j d", j=J)
                else:
                    dve.wait_ge(o_ready[c], n + 1)
                    o = bank(c, OUT)[:, 0:J * (d + 1)].rearrange("p (j d) -> p j d", j=J)
                nc.vector.reciprocal(inv[c][:, g % 2, :], o[:, :, d]).then_inc(inv_ready[c], 1)
                dve.wait_ge(inv_ready[c], n + 1)
                dst = o8[c][:, :, 16 * g:16 * g + 16] if narrow(a) else o64[c][:, g % 2, :, :]
                nc.vector.tensor_tensor(dst.rearrange("p b (h d) -> p h b d", h=2),
                                        o[:, :, 0:d].rearrange("p (h b) d -> p h b d", h=2),
                                        inv[c][:, g % 2, :].rearrange("p (h b) -> p h b", h=2).unsqueeze(3)
                                        .to_broadcast([P, 2, NB, d]), ALU.mult).then_inc(o_normed[c], 1)

            def glu(t, c, layer, f):
                dve.wait_ge(gate_ready[c], t * F + f + 1)
                at = layer * 2 * F + f
                nc.vector.scalar_tensor_tensor(out=hidden[c][:, f, :], in0=bank(c, PROJ + f % 2)[:, 0:W],
                                               scalar=small_part("h_b")[:, at:at + 1], in1=gate[c][:, f, :],
                                               op0=ALU.add, op1=ALU.mult).then_inc(glu_ready[c], 1)

            def add_residual(t, c, s, b):
                dve.wait_ge(y_ready[c], (t * SUBS + s) * NB + b + 1)
                dve.wait_ge(x_biased_ready[c], t * SUBS + s + 1)
                if s == SUBS - 1:
                    dve.wait_ge(stored[c], t * 16 + 16)
                    dst, done = x_out[c], out_ready[c]
                else:
                    dst, done = xs[c], x_ready[c]
                nc.vector.tensor_tensor(dst[:, b, :], bank(c, TURNED + b)[:, 0:P], x_biased[c][:, b, :], ALU.add
                                        ).then_inc(done, 1)

            def stream(t, c):
                dve.wait_ge(inputs_loaded[c], t * 32 + 32)
                each = NB * SUBS * 2
                nc.vector.tensor_copy(mod[c][:].rearrange("p b s k -> p (b s k)"),
                                      mods[:].rearrange("p b s k -> p (b s k)")[:, bass.ds((t * STREAMS + c) * each, each)]
                                      ).then_inc(mod_ready[c], 1)
                nc.vector.tensor_copy(xs[c][:], x_in[c][:]).then_inc(x_ready[c], NB)
                take_stats(t, c, 0, ctx_in[c])
                yield
                norm(t, c, 0, ctx_in[c], CD)
                yield
                for s in range(SUBS):
                    layer, kind = divmod(s, 3)
                    a = 2 * layer + kind
                    if s == 0:
                        dve.wait_ge(normedT_ready[c], (t * NORMS + 1) * NB)
                        dve.wait_ge(normed_ready[c], (t * NORMS + 1) * NB)
                        dve.wait_ge(x_ready[c], (t * SUBS + 1) * NB)
                        nc.vector.tensor_copy(stats[c][:, 0, 0:1], mean_var[c][:, 0, 0:1]).then_inc(inputs_taken[c], 1)
                        dve.wait_ge(inputs_taken[c], t + 1)
                    take_stats(t, c, 1 + s, xs[c], s)
                    yield
                    norm(t, c, 1 + s, xs[c], P)
                    yield
                    if kind == 2:
                        for pair in range(2):
                            if GLU[layer]:
                                glu(t, c, layer, 2 * pair)
                                glu(t, c, layer, 2 * pair + 1)
                            yield
                        yield
                        continue
                    if rotary(a):
                        rotate(t, c, a, 0)
                    take_v(t, c, a, 0)
                    yield
                    for i in range(G + LAGS):
                        if wide(a) and 0 <= i - 3 <= G - 3:
                            normalise(t, c, a, i - 3)
                        if rotary(a) and i + 1 < G:
                            rotate(t, c, a, i + 1)
                        if wide(a) and i == 0:
                            take_v(t, c, a, 1)
                        if i < G:
                            shift(t, c, a, i)
                        if narrow(a) and 0 <= i - 3 < G:
                            normalise(t, c, a, i - 3)
                        if wide(a) and G <= i < G + 2:
                            normalise(t, c, a, i - 2)
                        yield
                    if narrow(a):
                        yield
                    yield
                for b in range(NB):
                    add_residual(t, c, SUBS - 1, b)
                yield

            with dve.Fori(0, TURNS) as t:
                interleave(stream(t, 0), stream(t, 1))

        @block.tensor
        def _(pe):
            mm = nc.tensor.matmul
            pe.wait_ge(small_loaded, 16)
            pe.wait_ge(mod_w_loaded, 16)
            pe.wait_ge(silu_ready, 1)
            for n in range(2 * SUBS):
                src = cond_silu[:] if n // 6 in (0, 3) else small_part("cond")
                last = mm(ps[:, MOD_BANK, n * B:(n + 1) * B], mod_w[:, n * P:(n + 1) * P], src, start=True, stop=True)
            last.then_inc(mod_projected, 1)

            def turn_norm(t, c, n, width):
                for b in range(NB):
                    pe.wait_ge(normed_ready[c], (t * NORMS + n) * NB + b + 1)
                    nc.tensor.transpose(bank(c, PROJ + b)[0:width, 0:P], normed[c][:, b, 0:width], ident
                                        ).then_inc(normedT_ready[c], 1)

            def kv_source(c, a):
                if a % 2 == 0:
                    return hT[c], P
                return [(ctxT[c], CD), (ctx_normT[c], CD), (ctxT[c], CD), (ctx_projT[c], P)][a // 2]

            def project_qk(t, c, a, g):
                s, (kv, depth) = sub_of(a), kv_source(c, a)
                if g >= AHEAD + LAGS:
                    pe.wait_ge(oT_ready[c], at_ot(t, a, g - AHEAD - LAGS + 1))
                if g:
                    pe.wait_ge(qk_taken[c], at_qk(t, a, g))
                cols = slice(g * P, (g + 1) * P)
                mm(bank(c, PROJ)[:, 0:W], weight(s, "q")[:, cols], hT[c][:], start=True, stop=True)
                mm(bank(c, PROJ)[:, W:2 * W], weight(s, "k")[0:depth, cols], kv[0:depth, :],
                   start=True, stop=True).then_inc(qk_projected[c], 1)

            def project_v(t, c, a, part):
                s, (kv, depth) = sub_of(a), kv_source(c, a)
                if narrow(a):
                    for b in range(NB):
                        last = mm(bank(c, SCORE)[:, b * P:(b + 1) * P], kv[0:depth, b * P:(b + 1) * P],
                                  weight(s, "v")[0:depth, :], start=True, stop=True)
                else:
                    for b, half, where in (((0, 0, SCORE), (0, 1, TURNED), (1, 0, OUT)), ((1, 1, TURNED),))[part]:
                        last = mm(bank(c, where), kv[0:depth, b * P:(b + 1) * P],
                                  weight(s, "v")[0:depth, half * 512:(half + 1) * 512], start=True, stop=True)
                last.then_inc(v_projected[c], 1)

            def scores(t, c, a, g):
                n = group(t, a, g)
                if narrow(a):
                    pe.wait_ge(k_masked[c], at_narrow(t, a, g) + 1)
                elif rotary(a):
                    pe.wait_ge(k_split[c], at_rotated(t, a, g) + 1)
                else:
                    pe.wait_ge(qk_taken[c], at_qk(t, a, g) + 1)
                if g == 0:
                    pe.wait_ge(v_taken_dve[c], at_v(t, a, 1))
                    if wide(a):
                        pe.wait_ge(v_taken_act[c], at_wide(t, a) + 1)
                else:
                    pe.wait_ge(shifted_ready[c], n)
                for h in range(2):
                    for b in range(NB):
                        j = NB * h + b
                        last = mm(bank(c, SCORE)[:, j * P:(j + 1) * P],
                                  qk[c][:, 0 if narrow(a) else g % 2, b * P:(b + 1) * P],
                                  k_head[c][:, g % 2, h, b * P:(b + 1) * P], start=True, stop=True)
                last.then_inc(scores_ready[c], 1)

            def turn_shifted(t, c, a, g):
                n = group(t, a, g)
                if g == 0:
                    pe.wait_ge(v_taken_dve[c], at_v(t, a, v_parts(a)))
                else:
                    pe.wait_ge(probs_ready[c], n)
                pe.wait_ge(shifted_ready[c], n + 1)
                for j in range(J):
                    last = nc.tensor.transpose(bank(c, TURNED)[:, j * P:(j + 1) * P], shifted[c][:, g % 2, j, :], ident)
                last.then_inc(turned_ready[c], 1)

            def apply_probs(t, c, a, g):
                n = group(t, a, g)
                d = HEAD[a // 2]
                if g and narrow(a):
                    pe.wait_ge(o8T_ready[c], at_narrow(t, a, g))
                elif g:
                    pe.wait_ge(o_normed[c], n)
                pe.wait_ge(probs_ready[c], n + 1)
                for h in range(2):
                    for b in range(NB):
                        j = NB * h + b
                        probs = probsT[c][:, g % 2, j, :]
                        if narrow(a):
                            last = mm(bank(c, OUT)[j * V_ROWS:(j + 1) * V_ROWS, 0:P], v8[c][:, b, 2 * g + h, :], probs,
                                      start=True, stop=True)
                        else:
                            last = mm(bank(c, OUT)[:, j * (d + 1):(j + 1) * (d + 1)], probs, v64[c][:, b, 2 * g + h, :],
                                      start=True, stop=True)
                last.then_inc(o_ready[c], 1)

            def turn_o8(t, c, a, g):
                if g == 0:
                    pe.wait_ge(qk_taken[c], at_qk(t, a, 1))
                else:
                    pe.wait_ge(o_normed[c], group(t, a, g))
                pe.wait_ge(o8T_ready[c], at_narrow(t, a, g) + 1)
                nc.tensor.transpose(bank(c, PROJ)[:, 0:P], o8T[c][:, g % 2, :], ident).then_inc(o8_turned[c], 1)

            def turn_back(t, c, a, g):
                if wide(a):
                    pe.wait_ge(qk_taken[c], at_qk(t, a, min(g + LAGS + AHEAD, G)))
                    if g:
                        pe.wait_ge(oT_ready[c], at_ot(t, a, g))
                pe.wait_ge(o_normed[c], group(t, a, G if narrow(a) else g + 1))
                for b in range(NB):
                    src = o8[c][:, b, :] if narrow(a) else o64[c][:, g % 2, b, :]
                    last = nc.tensor.transpose(bank(c, PROJ)[:, b * P:(b + 1) * P], src, ident)
                last.then_inc(oT_turned[c], 1)

            def project_out(t, c, a):
                blocks = ot_count(a)
                pe.wait_ge(oT_ready[c], at_ot(t, a, blocks))
                for b in range(NB):
                    for g in range(blocks):
                        last = mm(bank(c, TURNED + b)[:, 0:P], oT[c][:, g, b, :], weight(sub_of(a), "o")[:, g * P:(g + 1) * P],
                                  start=(g == 0), stop=(g == blocks - 1))
                    last.then_inc(y_ready[c], 1)

            def mlp_up(t, c, layer, f):
                for i in range(2 if GLU[layer] else 1):
                    last = mm(bank(c, PROJ + f % 2)[:, i * W:(i + 1) * W],
                              weight(3 * layer + 2, "w1")[:, (i * F + f) * P:(i * F + f + 1) * P], hT[c][:], start=True, stop=True)
                last.then_inc(hidden_projected[c], 1)

            def mlp_down(t, c, layer, f):
                if GLU[layer]:
                    pe.wait_ge(glu_ready[c], t * F + f + 1)
                else:
                    done = F * sum(not GLU[i] for i in range(layer))
                    pe.wait_ge(hidden_ready[c], t * F * sum(not g for g in GLU) + done + f + 1)
                for b in range(NB):
                    last = mm(bank(c, TURNED + b)[:, 0:P], hidden[c][:, f, b * P:(b + 1) * P],
                              weight(3 * layer + 2, "w2")[:, f * P:(f + 1) * P], start=(f == 0), stop=(f == F - 1))
                    if f == F - 1:
                        last.then_inc(y_ready[c], 1)

            def stream(t, c):
                pe.wait_ge(inputs_loaded[c], t * 32 + 32)
                for b in range(NB):
                    last = nc.tensor.transpose(bank(c, SCORE)[0:CD, b * P:(b + 1) * P], ctx_in[c][:, b, :], ident)
                last.then_inc(ctx_taken[c], 1)
                yield
                pe.wait_ge(ctxT_ready[c], t + 1)
                mm(bank(c, TURNED)[:, 0:W], small_part("ctx_w")[0:CD, :], ctxT[c][:], start=True, stop=True
                   ).then_inc(ctx_projected[c], 1)
                turn_norm(t, c, 0, CD)
                yield
                for s in range(SUBS):
                    layer, kind = divmod(s, 3)
                    a = 2 * layer + kind
                    yield
                    if s == 0:
                        pe.wait_ge(ctx_projT_ready[c], t + 1)
                        pe.wait_ge(hT_ready[c], t * NORMS + 1)
                    turn_norm(t, c, 1 + s, P)
                    yield
                    pe.wait_ge(weights_loaded[s], 16)
                    pe.wait_ge(hT_ready[c], t * NORMS + s + 2)
                    if kind == 2:
                        mlp_up(t, c, layer, 0)
                        mlp_up(t, c, layer, 1)
                        yield
                        for f in (0, 1):
                            mlp_down(t, c, layer, f)
                        for f in (2, 3):
                            mlp_up(t, c, layer, f)
                        yield
                        for f in (2, 3):
                            mlp_down(t, c, layer, f)
                        yield
                        continue
                    project_qk(t, c, a, 0)
                    project_v(t, c, a, 0)
                    if wide(a):
                        project_qk(t, c, a, 1)
                    yield
                    for i in range(G + LAGS):
                        if wide(a) and i == 0:
                            pe.wait_ge(v_taken_act[c], at_wide(t, a) + 1)
                            project_v(t, c, a, 1)
                        if i < G:
                            scores(t, c, a, i)
                        if 0 <= i - 1 < G:
                            turn_shifted(t, c, a, i - 1)
                        if wide(a) and 0 <= i - 3 < G:
                            turn_back(t, c, a, i - 3)
                        if 0 <= i - 2 < G:
                            apply_probs(t, c, a, i - 2)
                        if wide(a) and i + AHEAD < G:
                            project_qk(t, c, a, i + AHEAD)
                        if narrow(a) and 0 <= i - 3 < G:
                            turn_o8(t, c, a, i - 3)
                        yield
                    if narrow(a):
                        turn_back(t, c, a, 0)
                        yield
                    project_out(t, c, a)
                    yield
                yield

            with pe.Fori(0, TURNS) as t:
                interleave(stream(t, 0), stream(t, 1))


def pack_weights(inputs):
    import numpy as np

    def rows(a):
        a = np.asarray(a)
        full = np.zeros((P, a.shape[1]), a.dtype)
        full[:a.shape[0]] = a
        return full

    def blocks(a):
        a = np.asarray(a)
        return a.reshape(-1, P, a.shape[1]).transpose(1, 0, 2).reshape(P, -1)

    L0, L1, L2, L3 = ({k[9:]: v for k, v in inputs.items() if k.startswith(f"L{i}_xcond_")} for i in range(4))
    q0, k0, v0 = np.split(np.asarray(L0["Wqkv"]), 3, axis=1)
    q3, k3, v3 = np.split(np.asarray(L3["W_qkv"]), 3, axis=1)
    sk, sv = np.split(np.asarray(L1["sa_wkv"]), 2, axis=1)
    ck, cv = np.split(np.asarray(L1["ca_wkv"]), 2, axis=1)
    parts = [
        [rows(q0), rows(k0), rows(v0), blocks(L0["Wos"])],
        [rows(L0["Wq"]), rows(L0["Wk"]), rows(L0["Wv"]), blocks(L0["Woc"])],
        [rows(L0["W1"]), blocks(L0["W2"])],
        [rows(L1["sa_wq"]), rows(sk), rows(sv), blocks(L1["sa_wo"])],
        [rows(L1["ca_wq"]), rows(ck), rows(cv), blocks(L1["ca_wo"])],
        [rows(L1["ff_w1"]), blocks(L1["ff_w2"])],
        [rows(L2["q1"]), rows(L2["k1"]), rows(L2["v1"]), blocks(L2["o1_w"])],
        [rows(L2["q2"]), rows(L2["k2"]), rows(L2["v2"]), blocks(L2["o2_w"])],
        [rows(L2["ff_w1"]), blocks(L2["ff_w2"])],
        [rows(q3), rows(k3), rows(v3), blocks(L3["W_proj"])],
        [rows(L3["W_q"]), rows(L3["W_k"]), rows(L3["W_v"]), blocks(L3["W_out"])],
        [rows(L3["W_fc1"]), blocks(L3["W_fc2"])],
    ]
    return [np.ascontiguousarray(np.concatenate(p, axis=1)) for p in parts]


def pack_small(inputs):
    import numpy as np

    L0, L1, L2, L3 = ({k[9:]: np.asarray(v) for k, v in inputs.items() if k.startswith(f"L{i}_xcond_")} for i in range(4))
    where, width = small_columns()
    full = np.zeros((P, width), np.float32)
    mod_w = np.zeros((P, 2 * SUBS * P), np.float32)

    def put(name, a, at=0):
        a = np.asarray(a)
        start = where[name][0] + at
        full[:a.shape[0], start:start + a.shape[1]] = a

    def cols(a):
        return np.asarray(a).reshape(-1, P).T

    def everywhere(a):
        return np.broadcast_to(np.asarray(a).reshape(1, -1), (P, np.asarray(a).size))

    put("ident", np.eye(P, dtype=np.float32))
    put("cond", np.asarray(inputs["cond_1024"]).T)
    m0, c0 = L0["Wmod"], L0["bmod"]
    m3, c3 = L3["W_ada"], L3["b_ada"]
    part = lambda a, i: a[..., i * P:(i + 1) * P]
    pairs = [(m0, c0, 1), (m0, c0, 0), (m0, c0, 3), (m0, c0, 2), (m0, c0, 5), (m0, c0, 4)]
    pairs += [(L1["g1_w"], L1["g1_b"], 0), (L1["b1_w"], L1["b1_b"], 0)] * 2
    pairs += [(L1["g2_w"], L1["g2_b"], 0), (L1["b2_w"], L1["b2_b"], 0)]
    for n in "123":
        pairs += [(L2[f"n{n}_w"], L2[f"n{n}_b"], 0), (L2[f"n{n}_w"], L2[f"n{n}_b"], 1)]
    pairs += [(m3, c3, 1), (m3, c3, 0), (m3, c3, 3), (m3, c3, 2), (m3, c3, 5), (m3, c3, 4)]
    for n, (w, b, i) in enumerate(pairs):
        mod_w[:, n * P:(n + 1) * P] = part(w, i)
        put("mod_b", cols(part(b, i)), n)
    norms = [("ln1", L0), ("ln2", L0), ("ln3", L0), ("ln1", L1), ("ln1", L1), ("ln2", L1)]
    for s in range(SUBS):
        if s < len(norms):
            name, layer = norms[s]
            put("ln_w", cols(layer[name + "_w"]), s)
            put("ln_b", cols(layer[name + "_b"]), s)
        else:
            put("ln_w", np.ones((P, 1), np.float32), s)
    put("ctx_w", L3["W_ctx"])
    put("ctx_b", cols(L3["b_ctx"]))
    put("ctx_ln_w", L1["ca_lnc_w"].reshape(CD, 1))
    put("ctx_ln_b", L1["ca_lnc_b"].reshape(CD, 1))
    d = 64
    inv_freq = np.float32(1.0) / np.float32(10000.0) ** (np.arange(0, d, 2, dtype=np.float32) / np.float32(d))
    angle = np.arange(P, dtype=np.float32)[None, :] * inv_freq[:, None]
    put("cos", np.tile(np.repeat(np.cos(angle), 2, axis=0), (2, 1)))
    put("sin", np.tile(np.stack([-np.sin(angle), np.sin(angle)], axis=1).reshape(d, P), (2, 1)))

    put("head_mask", np.repeat(np.eye(H, dtype=np.float32), P // H, axis=0))

    bq0, bk0, bv0 = np.split(L0["bqkv"], 3)
    bq3, bk3, bv3 = np.split(L3["b_qkv"], 3)
    for a, (bq, bk, bv) in {0: (bq0, bk0, bv0), 1: (L0["bq"], L0["bk"], L0["bv"]), 6: (bq3, bk3, bv3)}.items():
        put("qk_b", cols(bq), 2 * a)
        put("qk_b", cols(bk), 2 * a + 1)
        put("v_b", everywhere(bv), (a if a < 2 else a - 4) * P)
    outs = [L0["bos"], L0["boc"], L0["b2"], L1["sa_bo"], L1["ca_bo"], L1["ff_b2"],
            L2["o1_b"], L2["o2_b"], L2["ff_b2"], L3["b_proj"], L3["b_out"], L3["b_fc2"]]
    for s, b in enumerate(outs):
        put("out_b", everywhere(b), s * P)
    for layer, b in enumerate([L0["b1"], L1["ff_b1"], L2["ff_b1"], L3["b_fc1"]]):
        put("h_b", cols(b), layer * 2 * F)
    return full, mod_w


def kernel(**inputs):
    import numpy as np
    from concourse import bacc
    from concourse.bass_utils import run_bass_kernel_spmd

    arrays = {
        "x_dram": np.ascontiguousarray(inputs["x"]),
        "ctx_dram": np.ascontiguousarray(inputs["ctx_768"]),
    }
    arrays["small_dram"], arrays["mod_w_dram"] = pack_small(inputs)
    for s, w in enumerate(pack_weights(inputs)):
        arrays[f"weights{s}_dram"] = w
    nc = bacc.Bacc("TRN2", target_bir_lowering=False, num_devices=1)
    aps = {n: nc.dram_tensor(n, a.shape, mybir.dt.from_np(a.dtype), kind="ExternalInput").ap() for n, a in arrays.items()}
    out = nc.dram_tensor("out_dram", (B, P, P), F32, kind="ExternalOutput").ap()
    build(nc, aps["x_dram"], aps["ctx_dram"], aps["small_dram"], aps["mod_w_dram"],
          [aps[f"weights{s}_dram"] for s in range(SUBS)], out)
    r = run_bass_kernel_spmd(nc, [arrays], core_ids=[0])
    return r.results[0]["out_dram"]
```
